# Optimizing a Trainium2 kernel written in Bass

```python
import numpy as np
import jax
import jax.numpy as jnp

def _softmax(x, axis=-1):
    return jax.nn.softmax(x, axis=axis)

def _gelu(x):
    return jax.nn.gelu(x, approximate=True)

def _silu(x):
    return jax.nn.silu(x)

def _sigmoid(x):
    return jax.nn.sigmoid(x)

def _layernorm(x, axis=-1, eps=1e-05):
    m = jnp.mean(x, axis=axis, keepdims=True)
    v = jnp.var(x, axis=axis, keepdims=True)
    return (x - m) / jnp.sqrt(v + eps)

def _scatter_add(tgt, idx, src, axis=0):
    return tgt.at[idx].add(src)

def _segment_sum(src, seg, n):
    return jax.ops.segment_sum(src, seg, n)
kernel_name = 'mk_dlrm_tower_d1_rec_r8_aa7354'

def setup_inputs(seed: int=0):
    np.random.seed(seed)
    _w = jnp.asarray

    def _rec_inputs():
        import jax
        import jax.numpy as jnp
        _tk = jax.random.key(seed)
        dense_ctx = jax.random.normal(jax.random.fold_in(_tk, 190), (1024, 16), jnp.float32)
        ids = jnp.stack([jax.random.randint(jax.random.fold_in(_tk, 200 + f), (1024,), 0, v, jnp.int32) for f, v in enumerate([1000, 125000, 125000, 1250, 1000, 12500, 1250, 12500, 1000, 1250, 1000, 1250, 12500, 1250, 1000, 1250, 1250, 12500, 1000, 125000, 125000, 125000, 1250, 125000])], axis=1)
        tbl_0 = 0.05 * jax.random.normal(jax.random.fold_in(_tk, 500 + 0), (1000, 16), jnp.float32)
        tbl_1 = 0.05 * jax.random.normal(jax.random.fold_in(_tk, 500 + 1), (125000, 16), jnp.float32)
        tbl_2 = 0.05 * jax.random.normal(jax.random.fold_in(_tk, 500 + 2), (125000, 16), jnp.float32)
        tbl_3 = 0.05 * jax.random.normal(jax.random.fold_in(_tk, 500 + 3), (1250, 16), jnp.float32)
        tbl_4 = 0.05 * jax.random.normal(jax.random.fold_in(_tk, 500 + 4), (1000, 16), jnp.float32)
        tbl_5 = 0.05 * jax.random.normal(jax.random.fold_in(_tk, 500 + 5), (12500, 16), jnp.float32)
        tbl_6 = 0.05 * jax.random.normal(jax.random.fold_in(_tk, 500 + 6), (1250, 16), jnp.float32)
        tbl_7 = 0.05 * jax.random.normal(jax.random.fold_in(_tk, 500 + 7), (12500, 16), jnp.float32)
        tbl_8 = 0.05 * jax.random.normal(jax.random.fold_in(_tk, 500 + 8), (1000, 16), jnp.float32)
        tbl_9 = 0.05 * jax.random.normal(jax.random.fold_in(_tk, 500 + 9), (1250, 16), jnp.float32)
        tbl_10 = 0.05 * jax.random.normal(jax.random.fold_in(_tk, 500 + 10), (1000, 16), jnp.float32)
        tbl_11 = 0.05 * jax.random.normal(jax.random.fold_in(_tk, 500 + 11), (1250, 16), jnp.float32)
        tbl_12 = 0.05 * jax.random.normal(jax.random.fold_in(_tk, 500 + 12), (12500, 16), jnp.float32)
        tbl_13 = 0.05 * jax.random.normal(jax.random.fold_in(_tk, 500 + 13), (1250, 16), jnp.float32)
        tbl_14 = 0.05 * jax.random.normal(jax.random.fold_in(_tk, 500 + 14), (1000, 16), jnp.float32)
        tbl_15 = 0.05 * jax.random.normal(jax.random.fold_in(_tk, 500 + 15), (1250, 16), jnp.float32)
        tbl_16 = 0.05 * jax.random.normal(jax.random.fold_in(_tk, 500 + 16), (1250, 16), jnp.float32)
        tbl_17 = 0.05 * jax.random.normal(jax.random.fold_in(_tk, 500 + 17), (12500, 16), jnp.float32)
        tbl_18 = 0.05 * jax.random.normal(jax.random.fold_in(_tk, 500 + 18), (1000, 16), jnp.float32)
        tbl_19 = 0.05 * jax.random.normal(jax.random.fold_in(_tk, 500 + 19), (125000, 16), jnp.float32)
        tbl_20 = 0.05 * jax.random.normal(jax.random.fold_in(_tk, 500 + 20), (125000, 16), jnp.float32)
        tbl_21 = 0.05 * jax.random.normal(jax.random.fold_in(_tk, 500 + 21), (125000, 16), jnp.float32)
        tbl_22 = 0.05 * jax.random.normal(jax.random.fold_in(_tk, 500 + 22), (1250, 16), jnp.float32)
        tbl_23 = 0.05 * jax.random.normal(jax.random.fold_in(_tk, 500 + 23), (125000, 16), jnp.float32)
        _rk = jax.random.fold_in(_tk, 7)
        W_top1 = 0.0693375 * jax.random.normal(jax.random.fold_in(_tk, 801), (208, 512), jnp.float32)
        W_top2 = 0.0441942 * jax.random.normal(jax.random.fold_in(_tk, 802), (512, 256), jnp.float32)
        W_top3 = 0.0625 * jax.random.normal(jax.random.fold_in(_tk, 803), (256, 1), jnp.float32)
        b_top1 = jnp.zeros((512,), jnp.float32)
        b_top2 = jnp.zeros((256,), jnp.float32)
        return (dense_ctx, ids, tbl_0, tbl_1, tbl_2, tbl_3, tbl_4, tbl_5, tbl_6, tbl_7, tbl_8, tbl_9, tbl_10, tbl_11, tbl_12, tbl_13, tbl_14, tbl_15, tbl_16, tbl_17, tbl_18, tbl_19, tbl_20, tbl_21, tbl_22, tbl_23, W_top1, b_top1, W_top2, b_top2, W_top3)
    dense_ctx, ids, tbl_0, tbl_1, tbl_2, tbl_3, tbl_4, tbl_5, tbl_6, tbl_7, tbl_8, tbl_9, tbl_10, tbl_11, tbl_12, tbl_13, tbl_14, tbl_15, tbl_16, tbl_17, tbl_18, tbl_19, tbl_20, tbl_21, tbl_22, tbl_23, W_top1, b_top1, W_top2, b_top2, W_top3 = _rec_inputs()

    def _L0_rec_setup():
        import jax, jax.numpy as jnp
        import numpy as np
        B, F, D = (512, 24, 16)
        LAYER_SIZES = [64, 64, 64]

        def _cin_forward(X0, Ws):
            F_ = X0.shape[1]
            Xk = X0
            outs = []
            for W in Ws:
                H_prev = Xk.shape[1]
                Wr = W.reshape(F_, H_prev, W.shape[1])
                Xk = jnp.einsum('bfd,bhd,fho->bod', X0, Xk, Wr)
                outs.append(Xk.sum(axis=2))
            return jnp.concatenate(outs, axis=1)
        key = jax.random.key(seed)
        k0, k1, k2, k3 = jax.random.split(key, 4)
        X0 = jax.random.normal(k0, (B, F, D), dtype=jnp.float32)
        prev = F
        Ws = []
        for k, h in zip((k1, k2, k3), LAYER_SIZES):
            Ws.append(jax.random.normal(k, (prev * F, h), dtype=jnp.float32) * 0.01)
            prev = h
        return {'X0': X0, 'W0': Ws[0], 'W1': Ws[1], 'W2': Ws[2]}
    _L0_rec_all = _L0_rec_setup()
    _L0_rec_in = {k: v for k, v in _L0_rec_all.items() if k in ('W0', 'W1', 'W2')}
    del _L0_rec_all
    return {'dense_ctx': dense_ctx, 'ids': ids, 'tbl_0': tbl_0, 'tbl_1': tbl_1, 'tbl_2': tbl_2, 'tbl_3': tbl_3, 'tbl_4': tbl_4, 'tbl_5': tbl_5, 'tbl_6': tbl_6, 'tbl_7': tbl_7, 'tbl_8': tbl_8, 'tbl_9': tbl_9, 'tbl_10': tbl_10, 'tbl_11': tbl_11, 'tbl_12': tbl_12, 'tbl_13': tbl_13, 'tbl_14': tbl_14, 'tbl_15': tbl_15, 'tbl_16': tbl_16, 'tbl_17': tbl_17, 'tbl_18': tbl_18, 'tbl_19': tbl_19, 'tbl_20': tbl_20, 'tbl_21': tbl_21, 'tbl_22': tbl_22, 'tbl_23': tbl_23, 'W_top1': W_top1, 'b_top1': b_top1, 'W_top2': W_top2, 'b_top2': b_top2, 'W_top3': W_top3, 'L0_rec_W0': _L0_rec_in['W0'], 'L0_rec_W1': _L0_rec_in['W1'], 'L0_rec_W2': _L0_rec_in['W2']}

def reference(dense_ctx, ids, tbl_0, tbl_1, tbl_2, tbl_3, tbl_4, tbl_5, tbl_6, tbl_7, tbl_8, tbl_9, tbl_10, tbl_11, tbl_12, tbl_13, tbl_14, tbl_15, tbl_16, tbl_17, tbl_18, tbl_19, tbl_20, tbl_21, tbl_22, tbl_23, W_top1, b_top1, W_top2, b_top2, W_top3, L0_rec_W0, L0_rec_W1, L0_rec_W2):
    import jax
    import jax.numpy as jnp

    def _L0_rec_ref(X0, W0, W1, W2):
        import jax, jax.numpy as jnp
        import numpy as np
        B, F, D = (512, 24, 16)
        LAYER_SIZES = [64, 64, 64]

        def _cin_forward(X0, Ws):
            F_ = X0.shape[1]
            Xk = X0
            outs = []
            for W in Ws:
                H_prev = Xk.shape[1]
                Wr = W.reshape(F_, H_prev, W.shape[1])
                Xk = jnp.einsum('bfd,bhd,fho->bod', X0, Xk, Wr)
                outs.append(Xk.sum(axis=2))
            return jnp.concatenate(outs, axis=1)
        return _cin_forward(X0, (W0, W1, W2))
    e = jnp.stack([tbl_0[ids[:, 0]], tbl_1[ids[:, 1]], tbl_2[ids[:, 2]], tbl_3[ids[:, 3]], tbl_4[ids[:, 4]], tbl_5[ids[:, 5]], tbl_6[ids[:, 6]], tbl_7[ids[:, 7]], tbl_8[ids[:, 8]], tbl_9[ids[:, 9]], tbl_10[ids[:, 10]], tbl_11[ids[:, 11]], tbl_12[ids[:, 12]], tbl_13[ids[:, 13]], tbl_14[ids[:, 14]], tbl_15[ids[:, 15]], tbl_16[ids[:, 16]], tbl_17[ids[:, 17]], tbl_18[ids[:, 18]], tbl_19[ids[:, 19]], tbl_20[ids[:, 20]], tbl_21[ids[:, 21]], tbl_22[ids[:, 22]], tbl_23[ids[:, 23]]], axis=1)
    z = _L0_rec_ref(e, L0_rec_W0, L0_rec_W1, L0_rec_W2)
    z = z.reshape(z.shape[0], -1)
    h = jnp.concatenate([z, dense_ctx], axis=1)
    h = jnp.maximum(h @ W_top1 + b_top1, 0.0)
    h = jnp.maximum(h @ W_top2 + b_top2, 0.0)
    y = h @ W_top3
    return y

_drawn_inputs = setup_inputs


def setup_inputs(seed=0):
    import zlib

    import numpy as np

    out = dict(_drawn_inputs(seed))
    spreads = {'b_top1': (0.0, 0.1), 'b_top2': (0.0, 0.1)}
    factors = {'tbl_0': 8.0,
     'tbl_1': 8.0,
     'tbl_2': 8.0,
     'tbl_3': 8.0,
     'tbl_4': 8.0,
     'tbl_5': 8.0,
     'tbl_6': 8.0,
     'tbl_7': 8.0,
     'tbl_8': 8.0,
     'tbl_9': 8.0,
     'tbl_10': 8.0,
     'tbl_11': 8.0,
     'tbl_12': 8.0,
     'tbl_13': 8.0,
     'tbl_14': 8.0,
     'tbl_15': 8.0,
     'tbl_16': 8.0,
     'tbl_17': 8.0,
     'tbl_18': 8.0,
     'tbl_19': 8.0,
     'tbl_20': 8.0,
     'tbl_21': 8.0,
     'tbl_22': 8.0,
     'tbl_23': 8.0,
     'L0_rec_W0': 8.0,
     'L0_rec_W1': 8.0,
     'L0_rec_W2': 8.0}
    for name, (base, spread) in spreads.items():
        noise = np.random.default_rng([zlib.crc32(name.encode()), seed]).standard_normal(out[name].shape)
        drawn = base * np.exp(spread * noise) if base else spread * noise
        out[name] = jnp.asarray(drawn.astype(out[name].dtype))
    for name, factor in factors.items():
        out[name] = (out[name] * factor).astype(out[name].dtype)
    return out
```

```python
from contextlib import ExitStack

import numpy as np

import concourse.bass as bass
from concourse import mybir

F32 = mybir.dt.float32
BF16 = mybir.dt.bfloat16
I32 = mybir.dt.int32
ALU = mybir.AluOpType
ACT = mybir.ActivationFunctionType
AX_X = mybir.AxisListType.X

P = 128
B, F, D = 1024, 24, 16
H = 64
TILES = B // P
COLS = D * P
BLK = 512
HALF = 2 * BLK
PARTS = 3
FP = PARTS * F
N1 = 512
N2 = 256

JS = F // 2 + 1
J_CHUNK = P // F
L1_CHUNKS = -(-JS // J_CHUNK)
L1_ROWS = [F * min(J_CHUNK, JS - J_CHUNK * c) for c in range(L1_CHUNKS)]
COMMON_ROWS = J_CHUNK * F
L2_CHUNKS = F // 2

SEL_L2 = 0
SEL_L1 = SEL_L2 + L2_CHUNKS * P
SEL_COMMON = SEL_L1 + L1_CHUNKS * COMMON_ROWS
SEL_FIELDS = SEL_COMMON + COMMON_ROWS
SEL_COLS = SEL_FIELDS + F

L2_ITEMS = [("L2", c, h) for c in range(L2_CHUNKS) for h in range(2)]
L1_ITEMS = [[("L1", c, h) for c in range(L1_CHUNKS)] for h in range(2)]
L2_BEFORE, L2_BETWEEN = 14, 4
FULL = (L2_ITEMS[:L2_BEFORE] + L1_ITEMS[0] + L2_ITEMS[L2_BEFORE:L2_BEFORE + L2_BETWEEN] + L1_ITEMS[1]
        + L2_ITEMS[L2_BEFORE + L2_BETWEEN:])
PER_STEP = len(FULL)
FIRST_ITEMS = L1_ITEMS[0] + L1_ITEMS[1]
PRO = len(FIRST_ITEMS)
LAG = 3
PAIR_BUFS = 6
COMMON_AT = (11, 12)
SPLIT_AT = 5
SIDE = {5: ("x2t", 0), 6: ("x2t", 1), 7: ("xt", 0), 8: ("xt", 1), 10: ("gram", 0), 12: ("gram", 1),
        13: ("gram", 2), 15: ("gram", 3), 17: ("x0t", 0)}
SIDE_FIRST = {n: s for n, s in SIDE.items() if s[0] in ("xt", "x0t")}
SIDE_LAST = {n: s for n, s in SIDE.items() if s[0] != "xt"}
GK = 4
GROUPS = P // 8
NC = L2_CHUNKS + 1


def build_tower(nc, ids, tables, wide_w, wide_b, w0a, w0b, w1, w2, wt1a, wt1b, bt1, wt2, bt2, wt3, dense_t, sel_in,
                mask_in, ident_in, out):
    with ExitStack() as ctx:
        def sb(name, shape, dt=F32):
            return ctx.enter_context(nc.sbuf_tensor(name, shape, dt))

        def sem(name):
            return ctx.enter_context(nc.semaphore(name))

        sel_f = sb("sel_f", [FP, SEL_COLS])
        sel = sb("sel", [FP, SEL_COLS], BF16)
        mask = sb("mask", [P, 8])
        ident = sb("ident", [P, P])
        ident_b = sb("ident_b", [P, P], BF16)
        w0_a = sb("w0_a", [COMMON_ROWS, L1_CHUNKS, H])
        w0_b = sb("w0_b", [COMMON_ROWS, L1_CHUNKS, H])
        w0 = sb("w0", [COMMON_ROWS, L1_CHUNKS, H])
        w1_sb = sb("w1_sb", [P, L2_CHUNKS, H])
        w2_sb = sb("w2_sb", [P, L2_CHUNKS, H])
        wt1a_sb = sb("wt1a_sb", [P, N1])
        wt1b_sb = sb("wt1b_sb", [H + D, N1])
        wt2_sb = sb("wt2_sb", [P, N1 // P, N2])
        wt3_sb = sb("wt3_sb", [P, N2 // P])
        bt1_sb = sb("bt1_sb", [P, N1 // P])
        bt2_sb = sb("bt2_sb", [P, N2 // P])
        ids_sb = sb("ids_sb", [P, TILES, F], I32)
        emb = [sb(f"emb{s}", [P, F * D]) for s in range(2)]
        rest = sb("rest", [P, F * D])
        parts = sb("parts", [P, D, FP], BF16)
        x0parts = [sb(f"x0parts{s}", [FP, COLS], BF16) for s in range(2)]
        common = sb("common", [COMMON_ROWS, COLS])
        x1 = [sb(f"x1_{s}", [P, COLS]) for s in range(2)]
        pairs = [sb(f"pairs{s}", [P, HALF]) for s in range(PAIR_BUFS)]
        x2 = sb("x2", [H, COLS])
        x2t = sb("x2t", [P, GROUPS, H])
        x0diag = sb("x0diag", [P, GROUPS, 2, 8, NC])
        gram = sb("gram", [P, NC, B])
        z1 = sb("z1", [P, 2 * TILES, BLK // D])
        zin_b = sb("zin_b", [H + D, B])
        h2 = sb("h2", [P, N2 // P, B])
        y = sb("y", [1, B])

        def h1(m):
            return x1[m // 2][:, (m % 2) * B:(m % 2 + 1) * B]

        spread = [ctx.enter_context(nc.psum_tensor(f"spread{s}", [P, HALF], F32)) for s in range(2)]
        acc2 = ctx.enter_context(nc.psum_tensor("acc2", [P, 2, BLK], F32))
        acc1 = ctx.enter_context(nc.psum_tensor("acc1", [P, BLK], F32))
        misc = ctx.enter_context(nc.psum_tensor("misc", [P, BLK], F32))
        misc_b = misc[0:FP, :].bitcast(BF16)

        const_in = sem("const_in")
        mlp_in = sem("mlp_in")
        ids_in = sem("ids_in")
        const_done = sem("const_done")
        gathered = [sem(f"gathered{s}") for s in range(2)]
        split_step = sem("split_step")
        misc_ready = sem("misc_ready")
        misc_free = sem("misc_free")
        spread_ready = sem("spread_ready")
        common_done = sem("common_done")
        pairs_done = sem("pairs_done")
        main_done = sem("main_done")
        x1_done = sem("x1_done")
        z1_done = sem("z1_done")
        x2_done = sem("x2_done")
        z_ready = sem("z_ready")
        z_fold = sem("z_fold")
        z_copied = sem("z_copied")
        mlp_ready = sem("mlp_ready")
        mlp_done = sem("mlp_done")
        stored = sem("stored")

        def item(i, n):
            return PRO + PER_STEP * i + n

        def spreads(i, n):
            extra = sum(n > at for at in COMMON_AT) if False else sum(n >= at for at in COMMON_AT)
            return (2 + PRO) + (PER_STEP + 2) * i + n + extra

        def spreads_last(i, n):
            return (2 + PRO) + (PER_STEP + 2) * i + n

        def rounds(i):
            return 2 if isinstance(i, int) and i == 0 else 2 + len(SIDE_FIRST) + len(SIDE) * (i - 1)

        def side_of(i):
            if isinstance(i, int) and i == 0:
                return SIDE_FIRST
            if isinstance(i, int) and i == TILES - 1:
                return SIDE_LAST
            return SIDE

        def items_of(i):
            return L2_ITEMS if isinstance(i, int) and i == TILES - 1 else FULL

        def has_next(i):
            return not (isinstance(i, int) and i == TILES - 1)

        def has_last(i):
            return not (isinstance(i, int) and i == 0)

        def after(eng, s, value):
            if not (isinstance(value, int) and value <= 0):
                eng.wait_ge(s, value)

        def cols(h, half):
            return slice((2 * h + half) * BLK, (2 * h + half + 1) * BLK)

        def group_cols(t, k):
            return t[:, k * P:(k + 1) * P]

        def steps(eng, body):
            body(0, 0)
            with eng.Fori(0, (TILES - 2) // 2) as turn:
                body(turn * 2 + 1, 1)
                body(turn * 2 + 2, 0)
            body(TILES - 1, 1)

        block = ctx.enter_context(nc.Block())

        @block.sync
        def _(sp):
            sp.dma_start(ids_sb[:, :, :], ids.rearrange("(t p) f -> p t f", p=P)).then_inc(ids_in, 16)
            for dst, src in ((sel_f, sel_in), (ident, ident_in), (mask, mask_in), (w0_a, w0a), (w0_b, w0b),
                             (w1_sb, w1), (w2_sb, w2)):
                sp.dma_start(dst[:], src).then_inc(const_in, 16)
            for dst, src in ((wt1a_sb[:, :], wt1a), (wt1b_sb[:, :], wt1b), (wt2_sb[:, :, :], wt2), (wt3_sb[:, :], wt3),
                             (bt1_sb[:, :], bt1), (bt2_sb[:, :], bt2), (zin_b[H:H + D, :], dense_t)):
                sp.dma_start(dst, src).then_inc(mlp_in, 16)
            sp.wait_ge(mlp_done, 8 + 4 + 2)
            sp.dma_start(out.rearrange("b o -> o b"), y[:, :]).then_inc(stored, 16)
            sp.wait_ge(stored, 16)

        @block.gpsimd
        def _(pool):
            pool.wait_ge(ids_in, 16)
            for t in range(TILES):
                if t >= 2:
                    pool.wait_ge(split_step, 4 * (t - 1))
                e3 = emb[t % 2][:, :].rearrange("p (f d) -> p f d", f=F)
                for f in range(F):
                    pool.indirect_dma_start(
                        out=e3[:, f, :], out_offset=None, in_=tables[f],
                        in_offset=bass.IndirectOffsetOnAxis(ap=ids_sb[:, t, f:f + 1], axis=0),
                    ).then_inc(gathered[t % 2], 16)

        @block.vector
        def _(dve):
            dve.wait_ge(const_in, 16 * 7)
            dve.tensor_copy(sel[:, :], sel_f[:, :]).then_inc(const_done, 1)
            dve.tensor_copy(ident_b[:, :], ident[:, :]).then_inc(const_done, 1)
            dve.tensor_tensor(w0[:, :, :], w0_a[:, :, :], w0_b[:, :, :], ALU.add).then_inc(const_done, 1)
            for k in range(GROUPS):
                last = dve.tensor_copy(x0diag[:, k, :, :, L2_CHUNKS],
                                       mask[:, :].rearrange("p (a b) -> p a b", a=1).to_broadcast([P, 2, 8]))
            last.then_inc(const_done, 1)

            def split(t, slot, before):
                src = emb[slot][:, :].rearrange("p (f d) -> p d f", f=F)
                r = rest[:, :].rearrange("p (d f) -> p d f", f=F)
                dve.wait_ge(gathered[slot], (t - slot) * (8 * F) + 16 * F)
                after(dve, misc_ready, before)
                dve.tensor_copy(parts[:, :, 0:F], src).then_inc(split_step, 1)
                dve.wait_ge(split_step, 4 * t + 1)
                dve.tensor_tensor(r, src, parts[:, :, 0:F], ALU.subtract).then_inc(split_step, 1)
                dve.wait_ge(split_step, 4 * t + 2)
                dve.tensor_copy(parts[:, :, F:2 * F], r).then_inc(split_step, 1)
                dve.wait_ge(split_step, 4 * t + 3)
                dve.tensor_tensor(parts[:, :, 2 * F:3 * F], r, parts[:, :, F:2 * F], ALU.subtract)\
                    .then_inc(split_step, 1)

            def product(number, spread_number, what, slot, ring, buf):
                layer, c, h = what
                rows = P if layer == "L2" else L1_ROWS[c]
                other = x1[slot] if layer == "L2" else common
                after(dve, main_done, number - PAIR_BUFS + 1)
                dve.wait_ge(spread_ready, spread_number)
                dve.tensor_tensor(pairs[buf][0:rows, :], spread[ring][0:rows, :],
                                  other[0:rows, h * HALF:(h + 1) * HALF], ALU.mult).then_inc(pairs_done, 1)

            def sum_x1(tile, h):
                dve.tensor_reduce(z1[:, bass.ds(tile * 2 + h, 1), :].rearrange("p a (k r) -> p (a k) r", r=8),
                                  acc1[:, :].rearrange("p (k d r) -> p k r d", d=D, r=8),
                                  AX_X, ALU.add).then_inc(z1_done, 1)

            split(0, 0, 0)
            for n, what in enumerate(FIRST_ITEMS):
                dve.wait_ge(common_done, what[2] + 1)
                if n == 5:
                    dve.wait_ge(x1_done, 1)
                product(n, n + 3, what, 0, n % 2, n % PAIR_BUFS)
                if n == 5:
                    sum_x1(0, 0)

            z_at0 = [n for n, w in enumerate(FULL) if w[0] == "L1" and w[2] == 0][-1] + LAG + 3

            def body(i, slot):
                ring = 0
                for n, what in enumerate(items_of(i)):
                    layer, c, h = what
                    if n == SPLIT_AT and has_next(i):
                        x = [m for m, s in SIDE.items() if s == ("xt", 1)][0]
                        if has_last(i):
                            if isinstance(i, int) :
                                pass
                        split(i + 1, 1 - slot, last_transposes(i))
                    if c == 0 and layer == "L2":
                        dve.wait_ge(x1_done, 2 * i + h + 1)
                    if c == 0 and layer == "L1":
                        dve.wait_ge(common_done, 2 * (i + 1) + h + 1)
                    if n == z_at0 and has_next(i):
                        dve.wait_ge(x1_done, 2 * (i + 1) + 1)
                    seq = spreads(i, n) if has_next(i) else spreads_last(i, n)
                    ring = (n + (sum(n >= at for at in COMMON_AT) if has_next(i) else 0)) % 2
                    product(item(i, n), seq + 1, what, slot, ring, n % PAIR_BUFS)
                    if n == 1:
                        sum_x1(i, 1)
                    if n == z_at0 and has_next(i):
                        sum_x1(i + 1, 0)

            def last_transposes(i):
                if isinstance(i, int) and i == 0:
                    return 2
                order = [s for _, s in sorted(SIDE.items())]
                done = order.index(("xt", 1)) + 1
                if isinstance(i, int) and i == 1:
                    return 2 + 2
                return rounds(i) - len(SIDE) + done

            steps(dve, body)


        @block.scalar
        def _(act):
            def copy(dst, src):
                return act.activation(dst, src, ACT.Copy)

            def take(number, what, slot, i):
                kind, r = what
                act.wait_ge(misc_ready, number + 1)
                if kind == "xt":
                    copy(x0parts[1 - slot][:, :].rearrange("p (k d r) -> p d k r", d=D, r=8)[:, r * 8:(r + 1) * 8],
                         misc_b.rearrange("p (d k r) -> p d k r", d=8, r=8)).then_inc(misc_free, 1)
                elif kind == "x0t":
                    x0 = misc[:, 0:GROUPS * F].rearrange("p (k e c) -> p k e c", k=GROUPS, e=2)
                    for b in range(8):
                        last = act.activation(x0diag[:, :, :, b, 0:L2_CHUNKS], x0, ACT.Copy, scale=mask[:, b:b + 1])
                    last.then_inc(misc_free, 1)
                elif kind == "x2t":
                    copy(x2t[:, r * 8:(r + 1) * 8, :], misc[:, :].rearrange("p (k h) -> p k h", k=8))\
                        .then_inc(misc_free, 1)
                else:
                    at = (i - 1) * P + r * GK * 8
                    copy(gram[:, :, bass.ds(at, GK * 8)],
                         misc[:, 0:GK * 8 * NC].rearrange("p (b c) -> p c b", c=NC)).then_inc(misc_free, 1)

            def take_common(number, h):
                act.wait_ge(spread_ready, number + 1)
                copy(common[:, h * HALF:(h + 1) * HALF], spread[number_ring[0]][0:COMMON_ROWS, :])\
                    .then_inc(common_done, 1)

            number_ring = [0]

            def take_x1(last_item, h, slot):
                act.wait_ge(main_done, last_item + 1)
                for half in range(2):
                    for dup in range(2):
                        last = copy(x1[slot][dup * H:(dup + 1) * H, cols(h, half)], acc1[half * H:(half + 1) * H, :])
                last.then_inc(x1_done, 1)

            def take_x2(last_item, h):
                act.wait_ge(main_done, last_item + 1)
                for half in range(2):
                    last = copy(x2[:, cols(h, half)], acc2[half * H:(half + 1) * H, h, :])
                last.then_inc(x2_done, 1)

            act.wait_ge(const_in, 16 * 7)
            take(0, ("xt", 0), 1, 0)
            take(1, ("xt", 1), 1, 0)
            for h in range(2):
                number_ring[0] = h
                take_common(h, h)
            for h in range(2):
                take_x1(3 * h + 2, h, 0)

            def last_l1(h):
                return [n for n, w in enumerate(FULL) if w[0] == "L1" and w[2] == h][-1]

            def body(i, slot):
                side = side_of(i)
                if has_last(i):
                    take_x2(item(i, -2), 0)
                    take_x2(item(i, -1), 1)
                at = {}
                rnd = 0
                for n in range(len(items_of(i)) + LAG):
                    if n in side:
                        take(rounds(i) + rnd, side[n], slot, i)
                        rnd += 1
                    if has_next(i):
                        for h in range(2):
                            if n == COMMON_AT[h]:
                                number_ring[0] = (n + h) % 2
                                take_common(spreads(i, n) - 1 if h == 0 else spreads(i, n) - 1, h)
                        for h in range(2):
                            if n == last_l1(h) + LAG:
                                take_x1(item(i, last_l1(h)), h, 1 - slot)

            steps(act, body)

            act.wait_ge(main_done, item(TILES - 1, len(L2_ITEMS)))
            for h in range(2):
                for half in range(2):
                    last = copy(x2[:, cols(h, half)], acc2[half * H:(half + 1) * H, h, :])
                last.then_inc(x2_done, 1)
            base = rounds(TILES - 1) + len(SIDE_LAST)
            for r, what in enumerate([("x2t", 0), ("x2t", 1)] + [("gram", r) for r in range(4)]):
                take(base + r, what, 0, TILES)
            act.wait_ge(z1_done, 2 * TILES)
            for half in range(2):
                copy(zin_b[0:H, :].rearrange("p (t e b) -> p e t b", e=2, b=BLK // D)[:, half],
                     z1[half * H:(half + 1) * H, :, :]).then_inc(z_copied, 1)
            act.wait_ge(z_fold, 1)
            for b in range(2):
                copy(gram[H:P, L2_CHUNKS, b * BLK:(b + 1) * BLK], acc1[b * H:(b + 1) * H, :]).then_inc(z_copied, 1)
            for n in range(8):
                m, b = n // 2, n % 2
                act.wait_ge(mlp_ready, n + 1)
                if n == 0:
                    act.wait_ge(mlp_in, 16 * 7)
                act.activation(h1(m)[:, b * BLK:(b + 1) * BLK], spread[n % 2][:, 0:BLK], ACT.Relu,
                               bias=bt1_sb[:, m:m + 1]).then_inc(mlp_done, 1)
            for n in range(4):
                m, b = n // 2, n % 2
                act.wait_ge(mlp_ready, 8 + n + 1)
                act.activation(h2[:, m, b * BLK:(b + 1) * BLK], spread[n % 2][:, 0:BLK], ACT.Relu,
                               bias=bt2_sb[:, m:m + 1]).then_inc(mlp_done, 1)
            for b in range(2):
                act.wait_ge(mlp_ready, 12 + b + 1)
                copy(y[:, b * BLK:(b + 1) * BLK], spread[b][0:1, 0:BLK]).then_inc(mlp_done, 1)

        @block.tensor
        def _(pe):
            def spread_x0(number, first, rows, src, h, ring):
                for half in range(2):
                    last = pe.matmul(spread[ring][0:rows, half * BLK:(half + 1) * BLK], sel[:, first:first + rows],
                                     src[:, cols(h, half)], start=True, stop=True)
                last.then_inc(spread_ready, 1)

            def spread_item(number, what, x0, x0_next, ring):
                layer, c, h = what
                if layer == "L2":
                    spread_x0(number, SEL_L2 + c * P, P, x0, h, ring)
                else:
                    spread_x0(number, SEL_L1 + c * COMMON_ROWS, L1_ROWS[c], x0_next, h, ring)

            def contract(number, what, tile, buf):
                layer, c, h = what
                if c == 0 and layer == "L2":
                    after(pe, x2_done, 2 * (tile - 1) + h + 1)
                if c == 0 and layer == "L1":
                    after(pe, z1_done, 2 * tile + h)
                pe.wait_ge(pairs_done, number + 1)
                chunks = L2_CHUNKS if layer == "L2" else L1_CHUNKS
                for half in range(2):
                    rows = P if layer == "L2" else L1_ROWS[c]
                    w = w1_sb[:, c, :] if layer == "L2" else w0[0:rows, c, :]
                    acc = acc2[half * H:(half + 1) * H, h, :] if layer == "L2" else acc1[half * H:(half + 1) * H, :]
                    last = pe.matmul(acc, w, pairs[buf][0:rows, half * BLK:(half + 1) * BLK],
                                     start=(c == 0), stop=(c == chunks - 1))
                last.then_inc(main_done, 1)

            def side_waits(number, what, i):
                after(pe, misc_free, number)
                if what[0] == "x2t":
                    pe.wait_ge(x2_done, 2 * i)

            def side_round(number, what, slot, i):
                kind, r = what
                if kind == "xt":
                    pe.wait_ge(split_step, 4 * (i + 1) + 4)
                    for d in range(8):
                        last = pe.transpose(misc_b[:, d * P:(d + 1) * P], parts[:, r * 8 + d, :], ident_b[:, :])
                elif kind == "x0t":
                    for k in range(GROUPS):
                        last = pe.matmul(misc[:, k * F:(k + 1) * F], group_cols(x0parts[slot][:, :], k),
                                         sel[:, SEL_FIELDS:SEL_FIELDS + F], start=True, stop=True)
                elif kind == "x2t":
                    for k in range(8):
                        last = pe.transpose(misc[:, k * H:(k + 1) * H], group_cols(x2[:, :], r * 8 + k),
                                            ident[0:H, 0:H])
                else:
                    for k in range(GK):
                        for e in range(2):
                            last = pe.matmul(misc[e * H:(e + 1) * H, k * 8 * NC:(k + 1) * 8 * NC],
                                             x2t[:, r * GK + k, :], x0diag[:, r * GK + k, e, :, :],
                                             start=True, stop=True)
                last.then_inc(misc_ready, 1)

            pe.wait_ge(const_done, 4)
            side_round(0, ("xt", 0), 1, -1)
            side_waits(1, ("xt", 1), -1)
            side_round(1, ("xt", 1), 1, -1)
            pe.wait_ge(misc_free, 2)
            for h in range(2):
                spread_x0(h, SEL_COMMON, COMMON_ROWS, x0parts[0], h, h)
            for n, what in enumerate(FIRST_ITEMS):
                if n < 2:
                    pe.wait_ge(common_done, n + 1)
                else:
                    pe.wait_ge(pairs_done, n - 1)
                spread_item(2 + n, what, None, x0parts[0], n % 2)
                if n >= 2:
                    contract(n - 2, FIRST_ITEMS[n - 2], 0, (n - 2) % PAIR_BUFS)
            for n in range(PRO - 2, PRO):
                contract(n, FIRST_ITEMS[n], 0, n % PAIR_BUFS)

            def body(i, slot):
                side = side_of(i)
                items = items_of(i)
                rnd = 0
                freed = [("item", -2), ("item", -1)]
                for n, what in enumerate(items):
                    late = n in side and side[n][0] == "x2t"
                    if n in side:
                        side_waits(rounds(i) + rnd, side[n], i)
                        if not late:
                            side_round(rounds(i) + rnd, side[n], slot, i)
                    todo = [("common", h) for h in range(2) if has_next(i) and n == COMMON_AT[h]] + [("item", n)]
                    for kind, m in todo:
                        last_kind, last_m = freed.pop(0)
                        freed.append((kind, m))
                        seq = (spreads(i, n) if has_next(i) else spreads_last(i, n)) - (kind == "common")
                        ring = (n + (sum(n >= at for at in COMMON_AT) if has_next(i) else 0)
                                - (kind == "common")) % 2
                        if last_kind == "item":
                            pe.wait_ge(pairs_done, item(i, last_m) + 1)
                        else:
                            pe.wait_ge(common_done, 2 + 2 * i + last_m + 1)
                        if kind == "common":
                            if m == 0:
                                order = [s for _, s in sorted(side.items())]
                                pe.wait_ge(misc_free, rounds(i) + order.index(("xt", 1)) + 1)
                            spread_x0(seq, SEL_COMMON, COMMON_ROWS, x0parts[1 - slot], m, ring)
                        else:
                            spread_item(seq, what, x0parts[slot], x0parts[1 - slot], ring)
                    if late:
                        side_round(rounds(i) + rnd, side[n], slot, i)
                    rnd += n in side
                    if n >= LAG:
                        old = items[n - LAG]
                        contract(item(i, n - LAG), old, i if old[0] == "L2" else i + 1, (n - LAG) % PAIR_BUFS)
                    elif has_last(i):
                        contract(item(i, n - LAG), FULL[n - LAG], i - 1, (n - LAG) % PAIR_BUFS)

            steps(pe, body)
            count = len(L2_ITEMS)
            for n in range(count - LAG, count):
                contract(item(TILES - 1, n), L2_ITEMS[n], TILES - 1, n % PAIR_BUFS)

            pe.wait_ge(x2_done, 2 * TILES)
            base = rounds(TILES - 1) + len(SIDE_LAST)
            side_waits(base, ("x2t", 0), TILES)
            side_round(base, ("x2t", 0), 0, TILES)
            side_waits(base + 1, ("x2t", 1), TILES)
            side_round(base + 1, ("x2t", 1), 0, TILES)
            pe.wait_ge(misc_free, base + 2)
            for r in range(4):
                side_waits(base + 2 + r, ("gram", r), TILES)
                side_round(base + 2 + r, ("gram", r), 0, TILES)
            pe.wait_ge(misc_free, base + 6)
            for c in range(L2_CHUNKS):
                for b in range(2):
                    last = pe.matmul(acc1[b * H:(b + 1) * H, :], w2_sb[:, c, :], gram[:, c, b * BLK:(b + 1) * BLK],
                                     start=(c == 0), stop=(c == L2_CHUNKS - 1))
            last.then_inc(z_fold, 1)
            pe.wait_ge(mlp_in, 16 * 7)
            pe.wait_ge(z_copied, 4)
            for n in range(8):
                m, b = n // 2, n % 2
                if n >= 2:
                    pe.wait_ge(mlp_done, n - 1)
                bank = spread[n % 2][:, 0:BLK]
                pe.matmul(bank, wt1b_sb[:, m * P:(m + 1) * P], zin_b[:, b * BLK:(b + 1) * BLK], start=True, stop=False)
                pe.matmul(bank, wt1a_sb[:, m * P:(m + 1) * P], gram[:, L2_CHUNKS, b * BLK:(b + 1) * BLK],
                          start=False, stop=True).then_inc(mlp_ready, 1)
            pe.wait_ge(mlp_done, 8)
            for n in range(4):
                m, b = n // 2, n % 2
                if n >= 2:
                    pe.wait_ge(mlp_done, 8 + n - 1)
                for k in range(N1 // P):
                    last = pe.matmul(spread[n % 2][:, 0:BLK], wt2_sb[:, k, m * P:(m + 1) * P],
                                     h1(k)[:, b * BLK:(b + 1) * BLK], start=(k == 0), stop=(k == N1 // P - 1))
                last.then_inc(mlp_ready, 1)
            pe.wait_ge(mlp_done, 12)
            for b in range(2):
                for k in range(N2 // P):
                    last = pe.matmul(spread[b][0:1, 0:BLK], wt3_sb[:, k:k + 1], h2[:, k, b * BLK:(b + 1) * BLK],
                                     start=(k == 0), stop=(k == N2 // P - 1))
                last.then_inc(mlp_ready, 1)


def selectors():
    sel = np.zeros((PARTS, F, SEL_COLS), np.float32)
    for c in range(L2_CHUNKS):
        for m in range(P):
            sel[:, 2 * c + m // H, SEL_L2 + c * P + m] = 1
    for c in range(L1_CHUNKS):
        for m in range(L1_ROWS[c]):
            sel[:, (m % F + J_CHUNK * c + m // F) % F, SEL_L1 + c * COMMON_ROWS + m] = 1
    for m in range(COMMON_ROWS):
        sel[:, m % F, SEL_COMMON + m] = 1
    for m in range(F):
        sel[:, 2 * (m % L2_CHUNKS) + m // L2_CHUNKS, SEL_FIELDS + m] = 1
    return sel.reshape(FP, SEL_COLS)


def layer1_rows(w):
    w = w.reshape(F, F, H)
    a = np.zeros((L1_CHUNKS, J_CHUNK, F, H), w.dtype)
    b = np.zeros((L1_CHUNKS, J_CHUNK, F, H), w.dtype)
    for j in range(JS):
        for f in range(F):
            g = (f + j) % F
            a[j // J_CHUNK, j % J_CHUNK, f] = w[f, g]
            if 0 < j < F // 2:
                b[j // J_CHUNK, j % J_CHUNK, f] = w[g, f]
    return [np.ascontiguousarray(x.reshape(L1_CHUNKS, COMMON_ROWS, H).transpose(1, 0, 2)) for x in (a, b)]


def kernel(**inputs):
    import concourse.bacc as bacc
    from concourse.bass_utils import run_bass_kernel_spmd

    x = {k: np.asarray(v) for k, v in inputs.items()}
    w0a, w0b = layer1_rows(x["L0_rec_W0"])
    wt1 = x["W_top1"]
    group = np.arange(P)[:, None] % 8 == np.arange(8)[None, :]
    arrays = {
        "ids": x["ids"],
        "w0a": w0a,
        "w0b": w0b,
        "w1": x["L0_rec_W1"].reshape(L2_CHUNKS, P, H).transpose(1, 0, 2),
        "w2": x["L0_rec_W2"].reshape(L2_CHUNKS, P, H).transpose(1, 0, 2),
        "wt1a": wt1[H:3 * H],
        "wt1b": np.concatenate([wt1[0:H], wt1[3 * H:]]),
        "bt1": x["b_top1"].reshape(N1 // P, P).T,
        "wt2": x["W_top2"].reshape(N1 // P, P, N2).transpose(1, 0, 2),
        "bt2": x["b_top2"].reshape(N2 // P, P).T,
        "wt3": x["W_top3"].reshape(N2 // P, P).T,
        "dense_t": x["dense_ctx"].T,
        "sel": selectors(),
        "mask": group.astype(np.float32),
        "ident": np.eye(P, dtype=np.float32),
    }
    for f in range(F):
        arrays[f"tbl_{f}"] = x[f"tbl_{f}"]
    arrays = {k: np.ascontiguousarray(v) for k, v in arrays.items()}

    nc = bacc.Bacc("TRN2", target_bir_lowering=False, num_devices=1)
    ap = {k: nc.dram_tensor(f"in_{k}", v.shape, mybir.dt.from_np(v.dtype), kind="ExternalInput").ap()
          for k, v in arrays.items()}
    out = nc.dram_tensor("out_y", (B, 1), F32, kind="ExternalOutput").ap()
    build_tower(nc, ap["ids"], [ap[f"tbl_{f}"] for f in range(F)], None, None, ap["w0a"], ap["w0b"], ap["w1"],
                ap["w2"], ap["wt1a"], ap["wt1b"], ap["bt1"], ap["wt2"], ap["bt2"], ap["wt3"], ap["dense_t"],
                ap["sel"], ap["mask"], ap["ident"], out)
    got = run_bass_kernel_spmd(nc, [{f"in_{k}": v for k, v in arrays.items()}], core_ids=[0])
    return got.results[0]["out_y"]
```

```python
from contextlib import ExitStack

import numpy as np

import concourse.bass as bass
from concourse import mybir

F32 = mybir.dt.float32
BF16 = mybir.dt.bfloat16
I32 = mybir.dt.int32
ALU = mybir.AluOpType
ACT = mybir.ActivationFunctionType
AX_X = mybir.AxisListType.X

P = 128
B, F, D = 1024, 24, 16
H = 64
TILES = B // P
COLS = D * P
BLK = 512
HALF = 2 * BLK
PARTS = 3
FP = PARTS * F
N1 = 512
N2 = 256

JS = F // 2 + 1
J_CHUNK = P // F
L1_CHUNKS = -(-JS // J_CHUNK)
L1_ROWS = [F * min(J_CHUNK, JS - J_CHUNK * c) for c in range(L1_CHUNKS)]
COMMON_ROWS = J_CHUNK * F
L2_CHUNKS = F // 2

SEL_L2 = 0
SEL_L1 = SEL_L2 + L2_CHUNKS * P
SEL_COMMON = SEL_L1 + L1_CHUNKS * COMMON_ROWS
SEL_FIELDS = SEL_COMMON + COMMON_ROWS
SEL_COLS = SEL_FIELDS + F

L2_ITEMS = [("L2", c, h) for c in range(L2_CHUNKS) for h in range(2)]
L1_ITEMS = [[("L1", c, h) for c in range(L1_CHUNKS)] for h in range(2)]
L1_AT = [(12, 14, 15), (19, 20, 22)]


FIRST_CHUNKS = 4


def full_step(l2_items):
    places = {n: what for half, ns in zip(L1_ITEMS, L1_AT) for what, n in zip(half, ns)}
    rest = iter(l2_items)
    return [places[n] if n in places else next(rest) for n in range(len(L2_ITEMS) + len(places))]


FULL = full_step(L2_ITEMS)
FULL_FIRST = full_step([("L2", c, h) for h in range(2) for c in range(FIRST_CHUNKS)] + L2_ITEMS[2 * FIRST_CHUNKS:])
PER_STEP = len(FULL)
FIRST_ITEMS = L1_ITEMS[0] + L1_ITEMS[1]
PRO = len(FIRST_ITEMS)
LAG = 3
PAIR_BUFS = 6
AHEAD = 1
DMA_CHUNKS = [1, 3, 4, 5, 6, 7, 8, 9, 11]
DMA_BUFS = 3
COMMON_AT = (8, 9)
COMMON_AT_FIRST = (10, 11)
SPLIT_AT = 0
SPLIT_AT_FIRST = 4
SIDE = {4: ('xt', 0), 5: ('xt', 1), 6: ('x2t', 0), 8: ('x2t', 1), 12: ('gram', 0), 15: ('gram', 1), 18: ('gram', 2), 21: ('gram', 3), 22: ('x0t', 0)}
SIDE_FIRST = {7: ("xt", 0), 8: ("xt", 1), 22: ("x0t", 0)}
SIDE_LAST = {n: s for n, s in SIDE.items() if s[0] != "xt"}


def by_dma(what):
    return what[0] == "L2" and what[1] in DMA_CHUNKS


class Plan:

    def __init__(self, items, common_at, split_at, side):
        self.items, self.common_at, self.split_at, self.side = items, common_at, split_at, side
        uses = [(at, ("common", h)) for h, at in enumerate(common_at)]
        uses += [(max(0, n - AHEAD), ("item", n)) for n, what in enumerate(items) if not by_dma(what)]
        self.spreads = sorted(uses)
        self.uses = [use for _, use in self.spreads]
        self.l1_last = [max((n for n, w in enumerate(items) if w[0] == "L1" and w[2] == h), default=None)
                        for h in range(2)]


MIDDLE = Plan(FULL, COMMON_AT, SPLIT_AT, SIDE)
FIRST = Plan(FULL_FIRST, COMMON_AT_FIRST, SPLIT_AT_FIRST, SIDE_FIRST)
FINAL = Plan(L2_ITEMS, (), None, SIDE_LAST)
assert FIRST.uses[-2:] == MIDDLE.uses[-2:] and FIRST.items[-LAG:] == MIDDLE.items[-LAG:]

TAIL_ROUNDS = [("x2t", 0), ("x2t", 1)] + [("gram", r) for r in range(4)]
LAST = B - P
MLP_COLS = [(0, LAST // 2), (LAST // 2, LAST // 2), (LAST, P)]
GK = 4
GROUPS = P // 8
NC = L2_CHUNKS + 1


def build_tower(nc, ids, tables, w0a, w0b, w1, w2, wt1a, wt1b, bt1, wt2, bt2, wt3, dense_t, sel_in,
                mask_in, ident_in, out):
    with ExitStack() as ctx:
        def sb(name, shape, dt=F32):
            return ctx.enter_context(nc.sbuf_tensor(name, shape, dt))

        def sem(name):
            return ctx.enter_context(nc.semaphore(name))

        sel = sb("sel", [FP, SEL_COLS], BF16)
        mask = sb("mask", [P, 8])
        ident = sb("ident", [P, P])
        ident_b = sb("ident_b", [P, P], BF16)
        w0_a = sb("w0_a", [COMMON_ROWS, L1_CHUNKS, H])
        w0_b = sb("w0_b", [COMMON_ROWS, L1_CHUNKS, H])
        w0 = sb("w0", [COMMON_ROWS, L1_CHUNKS, H])
        w1_sb = sb("w1_sb", [P, L2_CHUNKS, H])
        w2_sb = sb("w2_sb", [P, L2_CHUNKS, H])
        wt1a_sb = sb("wt1a_sb", [P, N1])
        wt1b_sb = sb("wt1b_sb", [H + D, N1])
        wt2_sb = sb("wt2_sb", [P, N1 // P, N2])
        wt3_sb = sb("wt3_sb", [P, N2 // P])
        bt1_sb = sb("bt1_sb", [P, N1 // P])
        bt2_sb = sb("bt2_sb", [P, N2 // P])
        ids_sb = sb("ids_sb", [P, TILES, F], I32)
        emb = [sb(f"emb{s}", [P, F * D]) for s in range(2)]
        rest = sb("rest", [P, F * D])
        parts = sb("parts", [P, D, FP], BF16)
        x0parts = [sb(f"x0parts{s}", [FP, COLS], BF16) for s in range(2)]
        common = sb("common", [COMMON_ROWS, COLS])
        x1 = [sb(f"x1_{s}", [P, COLS]) for s in range(2)]
        spread_in = [sb(f"spread_in{s}", [P, COLS]) for s in range(DMA_BUFS)]
        pairs = [sb(f"pairs{s}", [P, HALF]) for s in range(PAIR_BUFS)]
        x2 = sb("x2", [P, 2, BLK])
        x2t = sb("x2t", [P, GROUPS, H])
        x0diag = sb("x0diag", [P, GROUPS, 2, 8, NC])
        gram = sb("gram", [P, NC, B])
        z1 = sb("z1", [P, 2 * TILES, BLK // D])
        zin_b = sb("zin_b", [H + D, B])
        h2 = sb("h2", [P, N2 // P, B])
        y = sb("y", [1, B])

        def h1(m):
            return x1[m // 2][:, (m % 2) * B:(m % 2 + 1) * B]

        def h2_rows(m):
            return h2[:, m, :]

        def bank(n):
            return spread[n // 2 % 2][:, n % 2 * BLK:(n % 2 + 1) * BLK]

        x0_dram = [nc.dram_tensor(f"x0_dram{s}", (F, COLS), F32).ap() for s in range(2)]

        spread = [ctx.enter_context(nc.psum_tensor(f"spread{s}", [P, HALF], F32)) for s in range(2)]
        acc2 = ctx.enter_context(nc.psum_tensor("acc2", [P, 2, BLK], F32))
        acc1 = ctx.enter_context(nc.psum_tensor("acc1", [P, BLK], F32))
        misc = ctx.enter_context(nc.psum_tensor("misc", [P, BLK], F32))
        misc_b = misc[0:FP, :].bitcast(BF16)
        acc1_b = acc1[0:FP, :].bitcast(BF16)

        const_in = sem("const_in")
        mlp_in = sem("mlp_in")
        ids_in = sem("ids_in")
        const_done = sem("const_done")
        gathered = [sem(f"gathered{s}") for s in range(2)]
        split_step = sem("split_step")
        misc_ready = sem("misc_ready")
        misc_free = sem("misc_free")
        spread_ready = sem("spread_ready")
        common_done = sem("common_done")
        x0_stored = [sem(f"x0_stored{s}") for s in range(2)]
        spread_landed = [sem(f"spread_landed{s}") for s in range(DMA_BUFS)]
        pairs_done = sem("pairs_done")
        main_done = sem("main_done")
        x1_done = sem("x1_done")
        z1_done = sem("z1_done")
        x2_done = sem("x2_done")
        z_ready = sem("z_ready")
        z_fold = sem("z_fold")
        z_copied = sem("z_copied")
        mlp_ready = sem("mlp_ready")
        mlp_done = sem("mlp_done")
        stored = sem("stored")

        def item(i, n):
            return PRO + PER_STEP * i + n

        def plan(i):
            return MIDDLE if not isinstance(i, int) else FIRST if i == 0 else FINAL if i == TILES - 1 else MIDDLE

        def spread_number(i, use):
            return (2 + PRO) + len(MIDDLE.uses) * i + plan(i).uses.index(use)

        def spread_slot(i, use):
            return plan(i).uses.index(use) % 2

        def rounds(i):
            return 2 if isinstance(i, int) and i == 0 else 2 + len(SIDE_FIRST) + len(SIDE) * (i - 1)

        def has_next(i):
            return not (isinstance(i, int) and i == TILES - 1)

        def has_last(i):
            return not (isinstance(i, int) and i == 0)

        def x1_bank(tile, h):
            return misc if isinstance(tile, int) and tile == 0 and h == 1 else acc1

        def after(eng, s, value):
            if not (isinstance(value, int) and value <= 0):
                eng.wait_ge(s, value)

        def cols(h, half):
            return slice((2 * h + half) * BLK, (2 * h + half + 1) * BLK)

        def group_cols(t, k):
            return t[:, k * P:(k + 1) * P]

        def steps(eng, body):
            body(0, 0)
            with eng.Fori(0, (TILES - 2) // 2) as turn:
                body(turn * 2 + 1, 1)
                body(turn * 2 + 2, 0)
            body(TILES - 1, 1)

        block = ctx.enter_context(nc.Block())

        @block.sync
        def _(sp):
            sp.dma_start(ids_sb[:, :, :], ids.rearrange("(t p) f -> p t f", p=P)).then_inc(ids_in, 16)
            for dst, src in ((sel, sel_in), (ident, ident_in), (mask, mask_in), (w0_a, w0a), (w0_b, w0b),
                             (w1_sb, w1), (w2_sb, w2)):
                sp.dma_start(dst[:], src).then_inc(const_in, 16)
            for dst, src in ((wt1a_sb[:, :], wt1a), (wt1b_sb[:, :], wt1b), (wt2_sb[:, :, :], wt2), (wt3_sb[:, :], wt3),
                             (bt1_sb[:, :], bt1), (bt2_sb[:, :], bt2), (zin_b[H:H + D, :], dense_t)):
                sp.dma_start(dst, src).then_inc(mlp_in, 16)
            def load_spread(j, i, slot):
                c, buf = DMA_CHUNKS[j], j % DMA_BUFS
                items = plan(i).items
                if j >= DMA_BUFS:
                    sp.wait_ge(pairs_done, item(i, items.index(("L2", DMA_CHUNKS[j - DMA_BUFS], 1))) + 1)
                elif has_last(i):
                    sp.wait_ge(pairs_done, item(i, FULL.index(("L2", DMA_CHUNKS[j - DMA_BUFS], 1)) - PER_STEP) + 1)
                if j == 0:
                    sp.wait_ge(x0_stored[slot], (i - slot) * 8 + 16)
                for e in range(2):
                    sp.dma_start(spread_in[buf][e * H:(e + 1) * H, :],
                                 x0_dram[slot][2 * c + e:2 * c + e + 1, :].to_broadcast([H, COLS]))\
                        .then_inc(spread_landed[buf], 16)

            def body(i, slot):
                for j in range(len(DMA_CHUNKS)):
                    load_spread(j, i, slot)

            steps(sp, body)
            sp.wait_ge(mlp_done, 3 * (N1 // P + N2 // P + 1))
            sp.dma_start(out.rearrange("b o -> o b"), y[:, :]).then_inc(stored, 16)
            sp.wait_ge(stored, 16)

        @block.gpsimd
        def _(pool):
            pool.wait_ge(ids_in, 16)
            for t in range(TILES):
                if t >= 2:
                    pool.wait_ge(split_step, 4 * (t - 1))
                e3 = emb[t % 2][:, :].rearrange("p (f d) -> p f d", f=F)
                for f in range(F):
                    pool.indirect_dma_start(
                        out=e3[:, f, :], out_offset=None, in_=tables[f],
                        in_offset=bass.IndirectOffsetOnAxis(ap=ids_sb[:, t, f:f + 1], axis=0),
                    ).then_inc(gathered[t % 2], 16)

        @block.vector
        def _(dve):
            dve.wait_ge(const_in, 16 * 7)
            dve.tensor_tensor(w0[:, :, :], w0_a[:, :, :], w0_b[:, :, :], ALU.add).then_inc(const_done, 1)
            for k in range(GROUPS):
                last = dve.tensor_copy(x0diag[:, k, :, :, L2_CHUNKS],
                                       mask[:, :].rearrange("p (a b) -> p a b", a=1).to_broadcast([P, 2, 8]))
            last.then_inc(const_done, 1)

            def split(t, slot, before):
                src = emb[slot][:, :].rearrange("p (f d) -> p d f", f=F)
                r = rest[:, :].rearrange("p (d f) -> p d f", f=F)
                dve.wait_ge(gathered[slot], (t - slot) * (8 * F) + 16 * F)
                after(dve, misc_ready, before)
                dve.tensor_copy(parts[:, :, 0:F], src).then_inc(split_step, 1)
                dve.wait_ge(split_step, 4 * t + 1)
                dve.tensor_tensor(r, src, parts[:, :, 0:F], ALU.subtract).then_inc(split_step, 1)
                dve.wait_ge(split_step, 4 * t + 2)
                dve.tensor_copy(parts[:, :, F:2 * F], r).then_inc(split_step, 1)
                dve.wait_ge(split_step, 4 * t + 3)
                dve.tensor_tensor(parts[:, :, 2 * F:3 * F], r, parts[:, :, F:2 * F], ALU.subtract)\
                    .then_inc(split_step, 1)

            def product(number, what, source, slot, buf):
                layer, c, h = what
                rows = P if layer == "L2" else L1_ROWS[c]
                other = x1[slot] if layer == "L2" else common
                after(dve, main_done, number - PAIR_BUFS + 1)
                dve.tensor_tensor(pairs[buf][0:rows, :], source[0:rows, :],
                                  other[0:rows, h * HALF:(h + 1) * HALF], ALU.mult).then_inc(pairs_done, 1)

            def sum_x1(tile, h):
                dve.tensor_reduce(z1[:, bass.ds(tile * 2 + h, 1), :].rearrange("p a (k r) -> p (a k) r", r=8),
                                  x1_bank(tile, h)[:, :].rearrange("p (k d r) -> p k r d", d=D, r=8),
                                  AX_X, ALU.add).then_inc(z1_done, 1)

            split(0, 0, 0)
            for n, what in enumerate(FIRST_ITEMS):
                dve.wait_ge(common_done, what[2] + 1)
                if n == 5:
                    dve.wait_ge(x1_done, 1)
                dve.wait_ge(spread_ready, 2 + n + 1)
                product(n, what, spread[n % 2], 0, n % PAIR_BUFS)
                if n == 5:
                    sum_x1(0, 0)

            def body(i, slot):
                z1_at = plan(i).l1_last[0] + LAG + 3 if has_next(i) else None
                for n, what in enumerate(plan(i).items):
                    layer, c, h = what
                    if n == plan(i).split_at:
                        split(i + 1, 1 - slot, last_transposes(i))
                    if c == 0 and layer == "L2":
                        dve.wait_ge(x1_done, 2 * i + h + 1)
                    if c == 0 and layer == "L1":
                        dve.wait_ge(common_done, 2 * (i + 1) + h + 1)
                    if n == z1_at:
                        dve.wait_ge(x1_done, 2 * (i + 1) + 1)
                    if by_dma(what):
                        j = DMA_CHUNKS.index(c)
                        source = spread_in[j % DMA_BUFS][:, h * HALF:(h + 1) * HALF]
                        landed = len(DMA_CHUNKS) // DMA_BUFS * i + j // DMA_BUFS + 1
                        dve.wait_ge(spread_landed[j % DMA_BUFS], 32 * landed)
                    else:
                        source = spread[spread_slot(i, ("item", n))]
                        dve.wait_ge(spread_ready, spread_number(i, ("item", n)) + 1)
                    product(item(i, n), what, source, slot, n % PAIR_BUFS)
                    if what == ("L2", 0, 1):
                        sum_x1(i, 1)
                    if n == z1_at:
                        sum_x1(i + 1, 0)

            def last_transposes(i):
                return 2 if isinstance(i, int) and i == 0 else rounds(i) - 1

            steps(dve, body)


        @block.scalar
        def _(act):
            def copy(dst, src):
                return act.activation(dst, src, ACT.Copy)

            def take(number, what, slot, i, bank_b=misc_b):
                kind, r = what
                act.wait_ge(misc_ready, number + 1)
                if kind == "xt":
                    copy(x0parts[1 - slot][:, :].rearrange("p (k d r) -> p d k r", d=D, r=8)[:, r * 8:(r + 1) * 8],
                         bank_b.rearrange("p (d k r) -> p d k r", d=8, r=8)).then_inc(misc_free, 1)
                elif kind == "x0t":
                    x0 = misc[:, 0:GROUPS * F].rearrange("p (k e c) -> p k e c", k=GROUPS, e=2)
                    for b in range(8):
                        last = act.activation(x0diag[:, :, :, b, 0:L2_CHUNKS], x0, ACT.Copy, scale=mask[:, b:b + 1])
                    last.then_inc(misc_free, 1)
                elif kind == "x2t":
                    copy(x2t[:, r * 8:(r + 1) * 8, :].rearrange("p (e k) h -> p k e h", e=2),
                         misc[:, :].rearrange("p (k e h) -> p k e h", k=4, e=2)).then_inc(misc_free, 1)
                else:
                    at = (i - 1) * P + r * GK * 8
                    copy(gram[:, :, bass.ds(at, GK * 8)],
                         misc[:, 0:GK * 8 * NC].rearrange("p (b c) -> p c b", c=NC)).then_inc(misc_free, 1)

            def take_common(number, buf, h, tile, slot):
                if h == 0:
                    after(act, x0_stored[1 - slot], (tile - 1 + slot) * 8)
                act.wait_ge(spread_ready, number + 1)
                copy(common[:, h * HALF:(h + 1) * HALF], spread[buf][0:COMMON_ROWS, :]).then_inc(common_done, 1)
                if h == 1:
                    act.wait_ge(common_done, 2 * tile + 2)
                    act.dma_start(x0_dram[slot], common[0:F, :]).then_inc(x0_stored[slot], 16)

            def take_x1(last_item, h, slot, bank):
                act.wait_ge(main_done, last_item + 1)
                for half in range(2):
                    for dup in range(2):
                        last = copy(x1[slot][dup * H:(dup + 1) * H, cols(h, half)], bank[half * H:(half + 1) * H, :])
                last.then_inc(x1_done, 1)

            def take_x2(last_item, h):
                act.wait_ge(main_done, last_item + 1)
                copy(x2[:, h, :], acc2[:, h, :]).then_inc(x2_done, 1)

            act.wait_ge(const_in, 16 * 7)
            copy(ident_b[:, :], ident[:, :]).then_inc(const_done, 1)
            take(0, ("xt", 0), 1, 0)
            take(1, ("xt", 1), 1, 0, acc1_b)
            for h in range(2):
                take_common(h, h, h, 0, 0)
            for h in range(2):
                take_x1(3 * h + 2, h, 0, x1_bank(0, h))

            def body(i, slot):
                side = plan(i).side
                if has_last(i):
                    take_x2(item(i, -2), 0)
                    take_x2(item(i, -1), 1)
                at = {}
                rnd = 0
                for n in range(len(plan(i).items) + LAG):
                    if n in side:
                        take(rounds(i) + rnd, side[n], slot, i)
                        rnd += 1
                    if has_next(i):
                        for h in range(2):
                            if n == plan(i).common_at[h]:
                                use = ("common", h)
                                take_common(spread_number(i, use), spread_slot(i, use), h, i + 1, 1 - slot)
                        for h in range(2):
                            if n == plan(i).l1_last[h] + LAG:
                                take_x1(item(i, plan(i).l1_last[h]), h, 1 - slot, acc1)

            steps(act, body)

            act.wait_ge(main_done, item(TILES - 1, len(L2_ITEMS)))
            for h in range(2):
                copy(x2[:, h, :], acc2[:, h, :]).then_inc(x2_done, 1)
            base = rounds(TILES - 1) + len(SIDE_LAST)
            act.wait_ge(z1_done, 2 * TILES)
            for half in range(2):
                copy(zin_b[0:H, :].rearrange("p (t e b) -> p e t b", e=2, b=BLK // D)[:, half],
                     z1[half * H:(half + 1) * H, :, :]).then_inc(z_copied, 1)
            for r, what in enumerate(TAIL_ROUNDS):
                take(base + r, what, 0, TILES)
            for b in range(2):
                copy(gram[H:P, L2_CHUNKS, bass.ds(*MLP_COLS[b])], acc1[b * H:(b + 1) * H, 0:MLP_COLS[b][1]])\
                    .then_inc(z_copied, 1)
            act.wait_ge(misc_ready, base + 7)
            copy(gram[H:P, L2_CHUNKS, bass.ds(*MLP_COLS[2])], misc[0:H, 0:MLP_COLS[2][1]]).then_inc(z_copied, 1)
            act.wait_ge(mlp_in, 16 * 7)
            outs = 0
            for layer, bias, count in ((h1, bt1_sb, N1 // P), (h2_rows, bt2_sb, N2 // P)):
                for at, n in MLP_COLS:
                    for m in range(count):
                        act.wait_ge(mlp_ready, outs + 1)
                        act.activation(layer(m)[:, at:at + n], bank(outs)[:, 0:n], ACT.Relu,
                                       bias=bias[:, m:m + 1]).then_inc(mlp_done, 1)
                        outs += 1
            for at, n in MLP_COLS:
                act.wait_ge(mlp_ready, outs + 1)
                copy(y[:, at:at + n], bank(outs)[0:1, 0:n]).then_inc(mlp_done, 1)
                outs += 1

        @block.tensor
        def _(pe):
            def spread_x0(first, rows, src, h, ring):
                for half in range(2):
                    last = pe.matmul(spread[ring][0:rows, half * BLK:(half + 1) * BLK], sel[:, first:first + rows],
                                     src[:, cols(h, half)], start=True, stop=True)
                last.then_inc(spread_ready, 1)

            def spread_item(what, x0, x0_next, ring):
                layer, c, h = what
                if layer == "L2":
                    spread_x0(SEL_L2 + c * P, P, x0, h, ring)
                else:
                    spread_x0(SEL_L1 + c * COMMON_ROWS, L1_ROWS[c], x0_next, h, ring)

            def contract(number, what, tile, buf):
                layer, c, h = what
                if c == 0 and layer == "L2":
                    after(pe, x2_done, 2 * (tile - 1) + h + 1)
                if c == 0 and layer == "L1" and not (isinstance(tile, int) and tile == 0):
                    pe.wait_ge(z1_done, 2 * tile + h)
                pe.wait_ge(pairs_done, number + 1)
                chunks = L2_CHUNKS if layer == "L2" else L1_CHUNKS
                for half in range(2):
                    rows = P if layer == "L2" else L1_ROWS[c]
                    w = w1_sb[:, c, :] if layer == "L2" else w0[0:rows, c, :]
                    acc = acc2[half * H:(half + 1) * H, h, :] if layer == "L2" else x1_bank(tile, h)[half * H:(half + 1) * H, :]
                    last = pe.matmul(acc, w, pairs[buf][0:rows, half * BLK:(half + 1) * BLK],
                                     start=(c == 0), stop=(c == chunks - 1))
                last.then_inc(main_done, 1)

            def side_waits(number, what, i):
                after(pe, misc_free, number)
                if what[0] == "x2t":
                    pe.wait_ge(x2_done, 2 * i)

            def side_round(number, what, slot, i, bank_b=misc_b):
                kind, r = what
                if kind == "xt":
                    pe.wait_ge(split_step, 4 * (i + 1) + 4)
                    for d in range(8):
                        last = pe.transpose(bank_b[:, d * P:(d + 1) * P], parts[:, r * 8 + d, :], ident_b[:, :])
                elif kind == "x0t":
                    for k in range(GROUPS):
                        last = pe.matmul(misc[:, k * F:(k + 1) * F], group_cols(x0parts[slot][:, :], k),
                                         sel[:, SEL_FIELDS:SEL_FIELDS + F], start=True, stop=True)
                elif kind == "x2t":
                    for k in range(4):
                        last = pe.transpose(misc[:, k * P:(k + 1) * P], group_cols(x2[:, r, :], k), ident[:, :])
                else:
                    for k in range(GK):
                        for e in range(2):
                            last = pe.matmul(misc[e * H:(e + 1) * H, k * 8 * NC:(k + 1) * 8 * NC],
                                             x2t[:, r * GK + k, :], x0diag[:, r * GK + k, e, :, :],
                                             start=True, stop=True)
                last.then_inc(misc_ready, 1)

            pe.wait_ge(const_done, 3)
            side_round(0, ("xt", 0), 1, -1)
            side_round(1, ("xt", 1), 1, -1, acc1_b)
            pe.wait_ge(misc_free, 2)
            for h in range(2):
                spread_x0(SEL_COMMON, COMMON_ROWS, x0parts[0], h, h)
            for n, what in enumerate(FIRST_ITEMS):
                if n < 2:
                    pe.wait_ge(common_done, n + 1)
                else:
                    pe.wait_ge(pairs_done, n - 1)
                spread_item(what, None, x0parts[0], n % 2)
                if n >= 2:
                    contract(n - 2, FIRST_ITEMS[n - 2], 0, (n - 2) % PAIR_BUFS)
            for n in range(PRO - 2, PRO):
                contract(n, FIRST_ITEMS[n], 0, n % PAIR_BUFS)

            def body(i, slot):
                side = plan(i).side
                items = plan(i).items
                rnd = 0
                uses = plan(i).spreads
                for n, what in enumerate(items):
                    late = n in side and side[n][0] == "x2t"
                    if n in side:
                        if not has_last(i) and rnd == 0:
                            pe.wait_ge(z1_done, 2)
                        side_waits(rounds(i) + rnd, side[n], i)
                        if not late:
                            side_round(rounds(i) + rnd, side[n], slot, i)
                    for q, (place, use) in enumerate(uses):
                        if place != n:
                            continue
                        if q < 2 and not has_last(i):
                            pe.wait_ge(pairs_done, item(i, q - 2) + 1)
                        elif q < 2:
                            pe.wait_ge(pairs_done, item(i, MIDDLE.uses[q - 2][1] - PER_STEP) + 1)
                        elif uses[q - 2][1][0] == "item":
                            pe.wait_ge(pairs_done, item(i, uses[q - 2][1][1]) + 1)
                        else:
                            pe.wait_ge(common_done, 2 + 2 * i + uses[q - 2][1][1] + 1)
                        buf = spread_slot(i, use)
                        if use[0] == "common":
                            if use[1] == 0:
                                order = [s for _, s in sorted(side.items())]
                                pe.wait_ge(misc_free, rounds(i) + order.index(("xt", 1)) + 1)
                            spread_x0(SEL_COMMON, COMMON_ROWS, x0parts[1 - slot], use[1], buf)
                        else:
                            spread_item(items[use[1]], x0parts[slot], x0parts[1 - slot], buf)
                    if n >= LAG:
                        old = items[n - LAG]
                        contract(item(i, n - LAG), old, i if old[0] == "L2" else i + 1, (n - LAG) % PAIR_BUFS)
                    elif has_last(i):
                        contract(item(i, n - LAG), FULL[n - LAG], i - 1, (n - LAG) % PAIR_BUFS)
                    if late:
                        side_round(rounds(i) + rnd, side[n], slot, i)
                    rnd += n in side

            steps(pe, body)
            count = len(L2_ITEMS)
            for n in range(count - LAG, count):
                contract(item(TILES - 1, n), L2_ITEMS[n], TILES - 1, n % PAIR_BUFS)

            base = rounds(TILES - 1) + len(SIDE_LAST)
            for c in range(L2_CHUNKS):
                for b in range(2):
                    last = pe.matmul(acc1[b * H:(b + 1) * H, 0:MLP_COLS[b][1]], w2_sb[:, c, :],
                                     gram[:, c, bass.ds(*MLP_COLS[b])], start=(c == 0), stop=(c == L2_CHUNKS - 1))
                if c % 2:
                    what = TAIL_ROUNDS[c // 2]
                    if what == ("gram", 0):
                        pe.wait_ge(misc_free, base + 2)
                    side_waits(base + c // 2, what, TILES)
                    side_round(base + c // 2, what, 0, TILES)
            pe.wait_ge(misc_free, base + 6)
            for c in range(L2_CHUNKS):
                last = pe.matmul(misc[0:H, 0:MLP_COLS[2][1]], w2_sb[:, c, :], gram[:, c, bass.ds(*MLP_COLS[2])],
                                 start=(c == 0), stop=(c == L2_CHUNKS - 1))
            last.then_inc(misc_ready, 1)
            pe.wait_ge(mlp_in, 16 * 7)
            outs = 0
            for g, (at, n) in enumerate(MLP_COLS):
                pe.wait_ge(z_copied, 2 + g + 1)
                for m in range(N1 // P):
                    after(pe, mlp_done, outs - 3)
                    pe.matmul(bank(outs)[:, 0:n], wt1b_sb[:, m * P:(m + 1) * P], zin_b[:, at:at + n],
                              start=True, stop=False)
                    pe.matmul(bank(outs)[:, 0:n], wt1a_sb[:, m * P:(m + 1) * P], gram[:, L2_CHUNKS, at:at + n],
                              start=False, stop=True).then_inc(mlp_ready, 1)
                    outs += 1
            for g, (at, n) in enumerate(MLP_COLS):
                for m in range(N2 // P):
                    pe.wait_ge(mlp_done, max(N1 // P * (g + 1), outs - 3))
                    for k in range(N1 // P):
                        last = pe.matmul(bank(outs)[:, 0:n], wt2_sb[:, k, m * P:(m + 1) * P], h1(k)[:, at:at + n],
                                         start=(k == 0), stop=(k == N1 // P - 1))
                    last.then_inc(mlp_ready, 1)
                    outs += 1
            for g, (at, n) in enumerate(MLP_COLS):
                pe.wait_ge(mlp_done, max(3 * N1 // P + N2 // P * (g + 1), outs - 3))
                for k in range(N2 // P):
                    last = pe.matmul(bank(outs)[0:1, 0:n], wt3_sb[:, k:k + 1], h2[:, k, at:at + n],
                                     start=(k == 0), stop=(k == N2 // P - 1))
                last.then_inc(mlp_ready, 1)
                outs += 1


def selectors():
    sel = np.zeros((PARTS, F, SEL_COLS), mybir.dt.np(BF16))
    for c in range(L2_CHUNKS):
        for m in range(P):
            sel[:, 2 * c + m // H, SEL_L2 + c * P + m] = 1
    for c in range(L1_CHUNKS):
        for m in range(L1_ROWS[c]):
            sel[:, (m % F + J_CHUNK * c + m // F) % F, SEL_L1 + c * COMMON_ROWS + m] = 1
    for m in range(COMMON_ROWS):
        sel[:, m % F, SEL_COMMON + m] = 1
    for m in range(F):
        sel[:, 2 * (m % L2_CHUNKS) + m // L2_CHUNKS, SEL_FIELDS + m] = 1
    return sel.reshape(FP, SEL_COLS)


def layer1_rows(w):
    w = w.reshape(F, F, H)
    a = np.zeros((L1_CHUNKS, J_CHUNK, F, H), w.dtype)
    b = np.zeros((L1_CHUNKS, J_CHUNK, F, H), w.dtype)
    for j in range(JS):
        for f in range(F):
            g = (f + j) % F
            a[j // J_CHUNK, j % J_CHUNK, f] = w[f, g]
            if 0 < j < F // 2:
                b[j // J_CHUNK, j % J_CHUNK, f] = w[g, f]
    return [np.ascontiguousarray(x.reshape(L1_CHUNKS, COMMON_ROWS, H).transpose(1, 0, 2)) for x in (a, b)]


def kernel(**inputs):
    import concourse.bacc as bacc
    from concourse.bass_utils import run_bass_kernel_spmd

    x = {k: np.asarray(v) for k, v in inputs.items()}
    w0a, w0b = layer1_rows(x["L0_rec_W0"])
    wt1 = x["W_top1"]
    group = np.arange(P)[:, None] % 8 == np.arange(8)[None, :]
    arrays = {
        "ids": x["ids"],
        "w0a": w0a,
        "w0b": w0b,
        "w1": x["L0_rec_W1"].reshape(L2_CHUNKS, P, H).transpose(1, 0, 2),
        "w2": x["L0_rec_W2"].reshape(L2_CHUNKS, P, H).transpose(1, 0, 2),
        "wt1a": wt1[H:3 * H],
        "wt1b": np.concatenate([wt1[0:H], wt1[3 * H:]]),
        "bt1": x["b_top1"].reshape(N1 // P, P).T,
        "wt2": x["W_top2"].reshape(N1 // P, P, N2).transpose(1, 0, 2),
        "bt2": x["b_top2"].reshape(N2 // P, P).T,
        "wt3": x["W_top3"].reshape(N2 // P, P).T,
        "dense_t": x["dense_ctx"].T,
        "sel": selectors(),
        "mask": group.astype(np.float32),
        "ident": np.eye(P, dtype=np.float32),
    }
    for f in range(F):
        arrays[f"tbl_{f}"] = x[f"tbl_{f}"]
    arrays = {k: np.ascontiguousarray(v) for k, v in arrays.items()}

    nc = bacc.Bacc("TRN2", target_bir_lowering=False, num_devices=1)
    ap = {k: nc.dram_tensor(f"in_{k}", v.shape, mybir.dt.from_np(v.dtype), kind="ExternalInput").ap()
          for k, v in arrays.items()}
    out = nc.dram_tensor("out_y", (B, 1), F32, kind="ExternalOutput").ap()
    build_tower(nc, ap["ids"], [ap[f"tbl_{f}"] for f in range(F)], ap["w0a"], ap["w0b"], ap["w1"],
                ap["w2"], ap["wt1a"], ap["wt1b"], ap["bt1"], ap["wt2"], ap["bt2"], ap["wt3"], ap["dense_t"],
                ap["sel"], ap["mask"], ap["ident"], out)
    got = run_bass_kernel_spmd(nc, [{f"in_{k}": v for k, v in arrays.items()}], core_ids=[0])
    return got.results[0]["out_y"]
```

```python
from contextlib import ExitStack

import numpy as np

import concourse.bass as bass
from concourse import mybir

F32 = mybir.dt.float32
BF16 = mybir.dt.bfloat16
I32 = mybir.dt.int32
ALU = mybir.AluOpType
ACT = mybir.ActivationFunctionType
AX_X = mybir.AxisListType.X

P = 128
B, F, D = 1024, 24, 16
H = 64
TILES = B // P
COLS = D * P
BLK = 512
HALF = 2 * BLK
PARTS = 3
FP = PARTS * F
N1 = 512
N2 = 256

JS = F // 2 + 1
J_CHUNK = P // F
L1_CHUNKS = -(-JS // J_CHUNK)
L1_ROWS = [F * min(J_CHUNK, JS - J_CHUNK * c) for c in range(L1_CHUNKS)]
COMMON_ROWS = J_CHUNK * F
L2_CHUNKS = F // 2

SEL_L1 = 0
SEL_COMMON = SEL_L1 + L1_CHUNKS * COMMON_ROWS
SEL_FIELDS = SEL_COMMON + COMMON_ROWS
SEL_COLS = SEL_FIELDS + F

L2_ITEMS = [("L2", c, h) for c in range(L2_CHUNKS) for h in range(2)]
L1_ITEMS = [[("L1", c, h) for c in range(L1_CHUNKS)] for h in range(2)]
L1_AT = [(10, 12, 13), (20, 22, 23)]


def full_step():
    places = {n: what for half, ns in zip(L1_ITEMS, L1_AT) for what, n in zip(half, ns)}
    rest = iter(L2_ITEMS)
    return [places[n] if n in places else next(rest) for n in range(len(L2_ITEMS) + len(places))]


FULL = full_step()
PER_STEP = len(FULL)
FIRST_ITEMS = L1_ITEMS[0] + L1_ITEMS[1]
PRO = len(FIRST_ITEMS)
LAG = 3
PAIR_BUFS = 6
AHEAD = 1
DMA_BUFS = 4
assert L2_CHUNKS % DMA_BUFS == 0
COMMON_AT = (6, 8)
COMMON_AT_FIRST = (9, 10)
SIDE = {3: ("xt", 0), 4: ("xt", 1), 6: ("x2t", 0), 9: ("x2t", 1), 11: ("gram", 0), 13: ("gram", 1),
        15: ("gram", 2), 17: ("gram", 3), 19: ("x0t", 0), 23: ("z3", 0)}
SIDE_FIRST = {6: ("xt", 0), 7: ("xt", 1), 23: ("x0t", 0)}
SIDE_LAST = {n: s for n, s in SIDE.items() if s[0] != "xt"}


class Plan:

    def __init__(self, items, common_at, side):
        self.items, self.common_at, self.side = items, common_at, side
        uses = [(at, ("common", h)) for h, at in enumerate(common_at)]
        uses += [(max(0, n - AHEAD), ("item", n)) for n, what in enumerate(items) if what[0] == "L1"]
        self.spreads = sorted(uses)
        self.uses = [use for _, use in self.spreads]
        self.l1_last = [max((n for n, w in enumerate(items) if w[0] == "L1" and w[2] == h), default=None)
                        for h in range(2)]


MIDDLE = Plan(FULL, COMMON_AT, SIDE)
FIRST = Plan(FULL, COMMON_AT_FIRST, SIDE_FIRST)
FINAL = Plan(L2_ITEMS, (), SIDE_LAST)
assert FIRST.uses[-2:] == MIDDLE.uses[-2:]

TAIL_ROUNDS = [("x2t", 0), ("x2t", 1)] + [("gram", r) for r in range(4)] + [("z3", 0)]
MLP_COLS = [(0, BLK), (BLK, B - P - BLK), (B - P, P)]
MLP_M = [N1 // P, N2 // P, 1]
MLP_OUTS = [(layer, g, m) for layer, g in ((0, 0), (0, 1), (1, 0), (0, 2), (1, 1), (2, 0), (1, 2), (2, 1), (2, 2))
            for m in range(MLP_M[layer])]
GK = 4
GROUPS = P // 8
NC = L2_CHUNKS + 1


def build_tower(nc, ids, tables, w0a, w0b, w1, w2, wt1a, wt1b, bt1, wt2, bt2, wt3, dense_t, sel_in,
                mask_in, ident_in, out):
    with ExitStack() as ctx:
        def sb(name, shape, dt=F32):
            return ctx.enter_context(nc.sbuf_tensor(name, shape, dt))

        def sem(name):
            return ctx.enter_context(nc.semaphore(name))

        sel = sb("sel", [FP, SEL_COLS], BF16)
        mask = sb("mask", [P, 8])
        ident = sb("ident", [P, P])
        ident_b = sb("ident_b", [P, P], BF16)
        w0_a = sb("w0_a", [COMMON_ROWS, L1_CHUNKS, H])
        w0_b = sb("w0_b", [COMMON_ROWS, L1_CHUNKS, H])
        w0 = sb("w0", [COMMON_ROWS, L1_CHUNKS, H])
        w1_sb = sb("w1_sb", [P, L2_CHUNKS, H])
        w2_sb = sb("w2_sb", [P, L2_CHUNKS, H])
        wt1a_sb = sb("wt1a_sb", [P, N1])
        wt1b_sb = sb("wt1b_sb", [H + D, N1])
        wt2_sb = sb("wt2_sb", [P, N1 // P, N2])
        wt3_sb = sb("wt3_sb", [P, N2 // P])
        bt1_sb = sb("bt1_sb", [P, N1 // P])
        bt2_sb = sb("bt2_sb", [P, N2 // P])
        ids_sb = sb("ids_sb", [P, TILES, F], I32)
        emb = [sb(f"emb{s}", [P, F * D]) for s in range(2)]
        rest = sb("rest", [P, F * D])
        parts = sb("parts", [P, D, FP], BF16)
        x0parts = [sb(f"x0parts{s}", [FP, COLS], BF16) for s in range(2)]
        common = sb("common", [COMMON_ROWS, COLS])
        x1 = [sb(f"x1_{s}", [P, COLS]) for s in range(2)]
        spread_in = [sb(f"spread_in{s}", [P, COLS]) for s in range(DMA_BUFS)]
        pairs = [sb(f"pairs{s}", [P, HALF]) for s in range(PAIR_BUFS)]
        x2 = sb("x2", [P, 2, BLK])
        x2t = sb("x2t", [P, GROUPS, H])
        x0diag = sb("x0diag", [P, GROUPS, 2, 8, NC])
        gram = sb("gram", [P, NC, P])
        z23 = sb("z23", [P, B])
        z1 = sb("z1", [P, 2 * TILES, BLK // D])
        zin_b = sb("zin_b", [H + D, B])
        h2 = sb("h2", [P, N2 // P, B])
        y = sb("y", [1, B])

        def h1(m):
            return x1[m // 2][:, (m % 2) * B:(m % 2 + 1) * B]

        def h2_rows(m):
            return h2[:, m, :]

        def bank(n):
            return spread[n // 2 % 2][:, n % 2 * BLK:(n % 2 + 1) * BLK]

        x0_dram = [nc.dram_tensor(f"x0_dram{s}", (F, COLS), F32).ap() for s in range(2)]

        spread = [ctx.enter_context(nc.psum_tensor(f"spread{s}", [P, HALF], F32)) for s in range(2)]
        acc2 = ctx.enter_context(nc.psum_tensor("acc2", [P, 2, BLK], F32))
        acc1 = ctx.enter_context(nc.psum_tensor("acc1", [P, BLK], F32))
        misc = ctx.enter_context(nc.psum_tensor("misc", [P, BLK], F32))
        xt_bank = [bank[0:FP, :].bitcast(BF16) for bank in (misc, acc1)]

        const_in = sem("const_in")
        mlp_in = sem("mlp_in")
        ids_in = sem("ids_in")
        const_done = sem("const_done")
        gathered = [sem(f"gathered{s}") for s in range(2)]
        split_step = sem("split_step")
        misc_ready = sem("misc_ready")
        misc_free = sem("misc_free")
        spread_ready = sem("spread_ready")
        common_done = sem("common_done")
        x0_stored = [sem(f"x0_stored{s}") for s in range(2)]
        spread_landed = [sem(f"spread_landed{s}") for s in range(DMA_BUFS)]
        pairs_done = sem("pairs_done")
        main_done = sem("main_done")
        x1_done = sem("x1_done")
        z1_done = sem("z1_done")
        x2_done = sem("x2_done")
        z1_copied = sem("z1_copied")
        mlp_ready = sem("mlp_ready")
        mlp_done = sem("mlp_done")
        stored = sem("stored")

        def item(i, n):
            return PRO + PER_STEP * i + n

        def plan(i):
            return MIDDLE if not isinstance(i, int) else FIRST if i == 0 else FINAL if i == TILES - 1 else MIDDLE

        def spread_number(i, use):
            return (2 + PRO) + len(MIDDLE.uses) * i + plan(i).uses.index(use)

        def spread_slot(i, use):
            return plan(i).uses.index(use) % 2

        def rounds(i):
            return 2 if isinstance(i, int) and i == 0 else 2 + len(SIDE_FIRST) + len(SIDE) * (i - 1)

        def last_transpose(i):
            return list(plan(i).side.values()).index(("xt", 1))

        def has_next(i):
            return not (isinstance(i, int) and i == TILES - 1)

        def has_last(i):
            return not (isinstance(i, int) and i == 0)

        def x1_bank(tile, h):
            return misc if isinstance(tile, int) and tile == 0 and h == 1 else acc1

        def after(eng, s, value):
            if not (isinstance(value, int) and value <= 0):
                eng.wait_ge(s, value)

        def cols(h, half):
            return slice((2 * h + half) * BLK, (2 * h + half + 1) * BLK)

        def group_cols(t, k):
            return t[:, k * P:(k + 1) * P]

        def steps(eng, body):
            body(0, 0)
            with eng.Fori(0, (TILES - 2) // 2) as turn:
                body(turn * 2 + 1, 1)
                body(turn * 2 + 2, 0)
            body(TILES - 1, 1)

        def split(eng, t):
            src = emb[t % 2][:, :].rearrange("p (f d) -> p d f", f=F)
            r = rest[:, :].rearrange("p (d f) -> p d f", f=F)
            eng.wait_ge(gathered[t % 2], (t // 2 + 1) * 16 * F)
            if t > 0:
                before = 2 if t == 1 else rounds(t - 2) + last_transpose(t - 2) + 1
                eng.wait_ge(misc_ready, before)
            eng.tensor_copy(parts[:, :, 0:F], src).then_inc(split_step, 1)
            eng.wait_ge(split_step, 4 * t + 1)
            eng.tensor_tensor(r, src, parts[:, :, 0:F], ALU.subtract).then_inc(split_step, 1)
            eng.wait_ge(split_step, 4 * t + 2)
            eng.tensor_copy(parts[:, :, F:2 * F], r).then_inc(split_step, 1)
            eng.wait_ge(split_step, 4 * t + 3)
            eng.tensor_tensor(parts[:, :, 2 * F:3 * F], r, parts[:, :, F:2 * F], ALU.subtract)\
                .then_inc(split_step, 1)

        block = ctx.enter_context(nc.Block())

        @block.sync
        def _(sp):
            sp.dma_start(ids_sb[:, :, :], ids.rearrange("(t p) f -> p t f", p=P)).then_inc(ids_in, 16)
            for dst, src in ((sel, sel_in), (ident, ident_in), (mask, mask_in), (w0_a, w0a), (w0_b, w0b),
                             (w1_sb, w1), (w2_sb, w2)):
                sp.dma_start(dst[:], src).then_inc(const_in, 16)
            for dst, src in ((wt1a_sb[:, :], wt1a), (wt1b_sb[:, :], wt1b), (wt2_sb[:, :, :], wt2), (wt3_sb[:, :], wt3),
                             (bt1_sb[:, :], bt1), (bt2_sb[:, :], bt2), (zin_b[H:H + D, :], dense_t)):
                sp.dma_start(dst, src).then_inc(mlp_in, 16)

            def body(i, slot):
                items = plan(i).items
                for c in range(L2_CHUNKS):
                    if c >= DMA_BUFS:
                        sp.wait_ge(pairs_done, item(i, items.index(("L2", c - DMA_BUFS, 1))) + 1)
                    elif has_last(i):
                        last_use = FULL.index(("L2", L2_CHUNKS + c - DMA_BUFS, 1)) - PER_STEP
                        sp.wait_ge(pairs_done, item(i, last_use) + 1)
                    if c == 0:
                        sp.wait_ge(x0_stored[slot], (i - slot) * 8 + 16)
                    for e in range(2):
                        sp.dma_start(spread_in[c % DMA_BUFS][e * H:(e + 1) * H, :],
                                     x0_dram[slot][2 * c + e:2 * c + e + 1, :].to_broadcast([H, COLS]))\
                            .then_inc(spread_landed[c % DMA_BUFS], 16)

            steps(sp, body)
            sp.wait_ge(mlp_done, len(MLP_OUTS))
            sp.dma_start(out.rearrange("b o -> o b"), y[:, :]).then_inc(stored, 16)
            sp.wait_ge(stored, 16)

        @block.gpsimd
        def _(pool):
            def gather(t):
                e3 = emb[t % 2][:, :].rearrange("p (f d) -> p f d", f=F)
                if t >= 2:
                    pool.wait_ge(split_step, 4 * (t - 1))
                for f in range(F):
                    pool.indirect_dma_start(
                        out=e3[:, f, :], out_offset=None, in_=tables[f],
                        in_offset=bass.IndirectOffsetOnAxis(ap=ids_sb[:, t, f:f + 1], axis=0),
                    ).then_inc(gathered[t % 2], 16)

            pool.wait_ge(ids_in, 16)
            gather(0)
            for t in range(1, TILES):
                gather(t)
                split(pool, t)

        @block.vector
        def _(dve):
            dve.wait_ge(const_in, 16 * 7)
            dve.tensor_tensor(w0[:, :, :], w0_a[:, :, :], w0_b[:, :, :], ALU.add).then_inc(const_done, 1)
            for k in range(GROUPS):
                last = dve.tensor_copy(x0diag[:, k, :, :, L2_CHUNKS],
                                       mask[:, :].rearrange("p (a b) -> p a b", a=1).to_broadcast([P, 2, 8]))
            last.then_inc(const_done, 1)

            def product(number, what, source, slot, buf):
                layer, c, h = what
                rows = P if layer == "L2" else L1_ROWS[c]
                other = x1[slot] if layer == "L2" else common
                after(dve, main_done, number - PAIR_BUFS + 1)
                dve.tensor_tensor(pairs[buf][0:rows, :], source[0:rows, :],
                                  other[0:rows, h * HALF:(h + 1) * HALF], ALU.mult).then_inc(pairs_done, 1)

            def sum_x1(tile, h):
                dve.tensor_reduce(z1[:, bass.ds(tile * 2 + h, 1), :].rearrange("p a (k r) -> p (a k) r", r=8),
                                  x1_bank(tile, h)[:, :].rearrange("p (k d r) -> p k r d", d=D, r=8),
                                  AX_X, ALU.add).then_inc(z1_done, 1)

            split(dve, 0)
            for n, what in enumerate(FIRST_ITEMS):
                dve.wait_ge(common_done, what[2] + 1)
                if n == 5:
                    dve.wait_ge(x1_done, 1)
                dve.wait_ge(spread_ready, 2 + n + 1)
                product(n, what, spread[n % 2], 0, n % PAIR_BUFS)
                if n == 5:
                    sum_x1(0, 0)

            def body(i, slot):
                z1_at = plan(i).l1_last[0] + LAG + 3 if has_next(i) else None
                for n, what in enumerate(plan(i).items):
                    layer, c, h = what
                    if c == 0 and layer == "L2":
                        dve.wait_ge(x1_done, 2 * i + h + 1)
                    if c == 0 and layer == "L1":
                        dve.wait_ge(common_done, 2 * (i + 1) + h + 1)
                    if n == z1_at:
                        dve.wait_ge(x1_done, 2 * (i + 1) + 1)
                    if layer == "L2":
                        source = spread_in[c % DMA_BUFS][:, h * HALF:(h + 1) * HALF]
                        dve.wait_ge(spread_landed[c % DMA_BUFS], 32 * (L2_CHUNKS // DMA_BUFS * i + c // DMA_BUFS + 1))
                    else:
                        source = spread[spread_slot(i, ("item", n))]
                        dve.wait_ge(spread_ready, spread_number(i, ("item", n)) + 1)
                    product(item(i, n), what, source, slot, n % PAIR_BUFS)
                    if what == ("L2", 0, 1):
                        sum_x1(i, 1)
                    if n == z1_at:
                        sum_x1(i + 1, 0)

            steps(dve, body)

        @block.scalar
        def _(act):
            def copy(dst, src):
                return act.activation(dst, src, ACT.Copy)

            def take(number, what, slot, i):
                kind, r = what
                act.wait_ge(misc_ready, number + 1)
                if kind == "xt":
                    copy(x0parts[1 - slot][:, :].rearrange("p (k d r) -> p d k r", d=D, r=8)[:, r * 8:(r + 1) * 8],
                         xt_bank[r].rearrange("p (d k r) -> p d k r", d=8, r=8)).then_inc(misc_free, 1)
                elif kind == "x0t":
                    x0 = misc[:, 0:GROUPS * F].rearrange("p (k e c) -> p k e c", k=GROUPS, e=2)
                    for b in range(8):
                        last = act.activation(x0diag[:, :, :, b, 0:L2_CHUNKS], x0, ACT.Copy, scale=mask[:, b:b + 1])
                    last.then_inc(misc_free, 1)
                elif kind == "x2t":
                    copy(x2t[:, r * 8:(r + 1) * 8, :].rearrange("p (e k) h -> p k e h", e=2),
                         misc[:, :].rearrange("p (k e h) -> p k e h", k=4, e=2)).then_inc(misc_free, 1)
                elif kind == "z3":
                    at = (i - 1) * P
                    act.wait_ge(misc_free, number)
                    copy(z23[0:H, bass.ds(at, P)], gram[0:H, L2_CHUNKS, :])
                    for b in range(2):
                        last = copy(z23[H:P, bass.ds(at + b * (P // 2), P // 2)], misc[b * H:(b + 1) * H, 0:P // 2])
                    last.then_inc(misc_free, 1)
                else:
                    copy(gram[:, :, r * GK * 8:(r + 1) * GK * 8],
                         misc[:, 0:GK * 8 * NC].rearrange("p (b c) -> p c b", c=NC)).then_inc(misc_free, 1)

            def take_common(number, buf, h, tile, slot):
                if h == 0:
                    after(act, x0_stored[1 - slot], (tile - 1 + slot) * 8)
                act.wait_ge(spread_ready, number + 1)
                copy(common[:, h * HALF:(h + 1) * HALF], spread[buf][0:COMMON_ROWS, :]).then_inc(common_done, 1)
                if h == 1:
                    act.wait_ge(common_done, 2 * tile + 2)
                    act.dma_start(x0_dram[slot], common[0:F, :]).then_inc(x0_stored[slot], 16)

            def take_x1(last_item, h, slot, bank):
                act.wait_ge(main_done, last_item + 1)
                for half in range(2):
                    for dup in range(2):
                        last = copy(x1[slot][dup * H:(dup + 1) * H, cols(h, half)], bank[half * H:(half + 1) * H, :])
                last.then_inc(x1_done, 1)

            def take_x2(last_item, h):
                act.wait_ge(main_done, last_item + 1)
                copy(x2[:, h, :], acc2[:, h, :]).then_inc(x2_done, 1)

            act.wait_ge(const_in, 16 * 7)
            copy(ident_b[:, :], ident[:, :]).then_inc(const_done, 1)
            take(0, ("xt", 0), 1, 0)
            take(1, ("xt", 1), 1, 0)
            for h in range(2):
                take_common(h, h, h, 0, 0)
            for h in range(2):
                take_x1(3 * h + 2, h, 0, x1_bank(0, h))

            def body(i, slot):
                side = plan(i).side
                if has_last(i):
                    take_x2(item(i, -2), 0)
                    take_x2(item(i, -1), 1)
                rnd = 0
                for n in range(len(plan(i).items) + LAG):
                    if n in side:
                        take(rounds(i) + rnd, side[n], slot, i)
                        rnd += 1
                    if has_next(i):
                        for h in range(2):
                            if n == plan(i).common_at[h]:
                                use = ("common", h)
                                take_common(spread_number(i, use), spread_slot(i, use), h, i + 1, 1 - slot)
                        for h in range(2):
                            if n == plan(i).l1_last[h] + LAG:
                                take_x1(item(i, plan(i).l1_last[h]), h, 1 - slot, acc1)

            steps(act, body)

            act.wait_ge(z1_done, 2 * TILES)
            for half in range(2):
                copy(zin_b[0:H, :].rearrange("p (t e b) -> p e t b", e=2, b=BLK // D)[:, half],
                     z1[half * H:(half + 1) * H, :, :]).then_inc(z1_copied, 1)
            act.wait_ge(mlp_in, 16 * 7)
            for h in range(2):
                take_x2(item(TILES - 1, len(L2_ITEMS) - 2 + h), h)
            base = rounds(TILES - 1) + len(SIDE_LAST)
            for o, (layer, g, m) in enumerate(MLP_OUTS):
                if o < len(TAIL_ROUNDS):
                    take(base + o, TAIL_ROUNDS[o], 0, TILES)
                at, n = MLP_COLS[g]
                act.wait_ge(mlp_ready, o + 1)
                if layer == 2:
                    for b in range(2):
                        last = copy(y[:, at + b * n // 2:at + (b + 1) * n // 2], bank(o)[b * H:b * H + 1, 0:n // 2])
                    last.then_inc(mlp_done, 1)
                else:
                    hidden, bias = ((h1, bt1_sb), (h2_rows, bt2_sb))[layer]
                    act.activation(hidden(m)[:, at:at + n], bank(o)[:, 0:n], ACT.Relu,
                                   bias=bias[:, m:m + 1]).then_inc(mlp_done, 1)

        @block.tensor
        def _(pe):
            def spread_x0(first, rows, src, h, ring):
                for half in range(2):
                    last = pe.matmul(spread[ring][0:rows, half * BLK:(half + 1) * BLK], sel[:, first:first + rows],
                                     src[:, cols(h, half)], start=True, stop=True)
                last.then_inc(spread_ready, 1)

            def spread_item(what, x0_next, ring):
                _, c, h = what
                spread_x0(SEL_L1 + c * COMMON_ROWS, L1_ROWS[c], x0_next, h, ring)

            def contract(number, what, tile, buf):
                layer, c, h = what
                if c == 0 and layer == "L2":
                    after(pe, x2_done, 2 * (tile - 1) + h + 1)
                if c == 0 and layer == "L1" and not (isinstance(tile, int) and tile == 0):
                    pe.wait_ge(z1_done, 2 * tile + h)
                pe.wait_ge(pairs_done, number + 1)
                chunks = L2_CHUNKS if layer == "L2" else L1_CHUNKS
                for half in range(2):
                    rows = P if layer == "L2" else L1_ROWS[c]
                    w = w1_sb[:, c, :] if layer == "L2" else w0[0:rows, c, :]
                    acc = acc2[:, h, :] if layer == "L2" else x1_bank(tile, h)
                    last = pe.matmul(acc[half * H:(half + 1) * H, :], w, pairs[buf][0:rows, half * BLK:(half + 1) * BLK],
                                     start=(c == 0), stop=(c == chunks - 1))
                last.then_inc(main_done, 1)

            def side_waits(number, what, i):
                if what == ("xt", 1):
                    pe.wait_ge(z1_done, 2 * i + 2)
                else:
                    after(pe, misc_free, number)
                if what[0] == "x2t":
                    pe.wait_ge(x2_done, 2 * i)

            def side_round(what, slot, i):
                kind, r = what
                if kind == "xt":
                    pe.wait_ge(split_step, 4 * (i + 1) + 4)
                    for d in range(8):
                        last = pe.transpose(xt_bank[r][:, d * P:(d + 1) * P], parts[:, r * 8 + d, :], ident_b[:, :])
                elif kind == "x0t":
                    for k in range(GROUPS):
                        last = pe.matmul(misc[:, k * F:(k + 1) * F], group_cols(x0parts[slot][:, :], k),
                                         sel[:, SEL_FIELDS:SEL_FIELDS + F], start=True, stop=True)
                elif kind == "x2t":
                    for k in range(4):
                        last = pe.transpose(misc[:, k * P:(k + 1) * P], group_cols(x2[:, r, :], k), ident[:, :])
                elif kind == "z3":
                    for c in range(L2_CHUNKS):
                        for b in range(2):
                            last = pe.matmul(misc[b * H:(b + 1) * H, 0:P // 2], w2_sb[:, c, :],
                                             gram[:, c, b * (P // 2):(b + 1) * (P // 2)],
                                             start=(c == 0), stop=(c == L2_CHUNKS - 1))
                else:
                    for k in range(GK):
                        for e in range(2):
                            last = pe.matmul(misc[e * H:(e + 1) * H, k * 8 * NC:(k + 1) * 8 * NC],
                                             x2t[:, r * GK + k, :], x0diag[:, r * GK + k, e, :, :],
                                             start=True, stop=True)
                last.then_inc(misc_ready, 1)

            pe.wait_ge(const_done, 3)
            side_round(("xt", 0), 1, -1)
            side_round(("xt", 1), 1, -1)
            pe.wait_ge(misc_free, 2)
            for h in range(2):
                spread_x0(SEL_COMMON, COMMON_ROWS, x0parts[0], h, h)
            for n, what in enumerate(FIRST_ITEMS):
                if n < 2:
                    pe.wait_ge(common_done, n + 1)
                else:
                    pe.wait_ge(pairs_done, n - 1)
                spread_item(what, x0parts[0], n % 2)
                if n >= LAG:
                    contract(n - LAG, FIRST_ITEMS[n - LAG], 0, (n - LAG) % PAIR_BUFS)
            for n in range(PRO - LAG, PRO):
                contract(n, FIRST_ITEMS[n], 0, n % PAIR_BUFS)

            def body(i, slot):
                side = plan(i).side
                items = plan(i).items
                rnd = 0
                uses = plan(i).spreads
                for n, what in enumerate(items):
                    late = n in side and side[n][0] == "x2t"
                    if n in side:
                        if not has_last(i) and rnd == 0:
                            pe.wait_ge(z1_done, 2)
                        side_waits(rounds(i) + rnd, side[n], i)
                        if not late:
                            side_round(side[n], slot, i)
                    for q, (place, use) in enumerate(uses):
                        if place != n:
                            continue
                        if q < 2 and not has_last(i):
                            pe.wait_ge(pairs_done, item(i, q - 2) + 1)
                        elif q < 2:
                            pe.wait_ge(pairs_done, item(i, MIDDLE.uses[q - 2][1] - PER_STEP) + 1)
                        elif uses[q - 2][1][0] == "item":
                            pe.wait_ge(pairs_done, item(i, uses[q - 2][1][1]) + 1)
                        else:
                            pe.wait_ge(common_done, 2 + 2 * i + uses[q - 2][1][1] + 1)
                        buf = spread_slot(i, use)
                        if use[0] == "common":
                            if use[1] == 0:
                                pe.wait_ge(misc_free, rounds(i) + last_transpose(i) + 1)
                            spread_x0(SEL_COMMON, COMMON_ROWS, x0parts[1 - slot], use[1], buf)
                        else:
                            spread_item(items[use[1]], x0parts[1 - slot], buf)
                    if n >= LAG:
                        old = items[n - LAG]
                        contract(item(i, n - LAG), old, i if old[0] == "L2" else i + 1, (n - LAG) % PAIR_BUFS)
                    elif has_last(i):
                        contract(item(i, n - LAG), FULL[n - LAG], i - 1, (n - LAG) % PAIR_BUFS)
                    if late:
                        side_round(side[n], slot, i)
                    rnd += n in side

            steps(pe, body)
            count = len(L2_ITEMS)
            for n in range(count - LAG, count):
                contract(item(TILES - 1, n), L2_ITEMS[n], TILES - 1, n % PAIR_BUFS)

            base = rounds(TILES - 1) + len(SIDE_LAST)
            pe.wait_ge(mlp_in, 16 * 7)
            pe.wait_ge(z1_copied, 2)
            for o, (layer, g, m) in enumerate(MLP_OUTS):
                if o < len(TAIL_ROUNDS):
                    side_waits(base + o, TAIL_ROUNDS[o], TILES)
                    side_round(TAIL_ROUNDS[o], 0, TILES)
                at, n = MLP_COLS[g]
                if layer == 0 and g == 2:
                    pe.wait_ge(misc_free, base + len(TAIL_ROUNDS))
                after(pe, mlp_done, o - 3)
                if layer > 0:
                    pe.wait_ge(mlp_done, MLP_OUTS.index((layer - 1, g, MLP_M[layer - 1] - 1)) + 1)
                if layer == 0:
                    pe.matmul(bank(o)[:, 0:n], wt1b_sb[:, m * P:(m + 1) * P], zin_b[:, at:at + n],
                              start=True, stop=False)
                    last = pe.matmul(bank(o)[:, 0:n], wt1a_sb[:, m * P:(m + 1) * P], z23[:, at:at + n],
                                     start=False, stop=True)
                elif layer == 1:
                    for k in range(N1 // P):
                        last = pe.matmul(bank(o)[:, 0:n], wt2_sb[:, k, m * P:(m + 1) * P], h1(k)[:, at:at + n],
                                         start=(k == 0), stop=(k == N1 // P - 1))
                else:
                    for k in range(N2 // P):
                        for b in range(2):
                            last = pe.matmul(bank(o)[b * H:b * H + 1, 0:n // 2], wt3_sb[:, k:k + 1],
                                             h2[:, k, at + b * n // 2:at + (b + 1) * n // 2],
                                             start=(k == 0), stop=(k == N2 // P - 1))
                last.then_inc(mlp_ready, 1)


def selectors():
    sel = np.zeros((PARTS, F, SEL_COLS), mybir.dt.np(BF16))
    for c in range(L1_CHUNKS):
        for m in range(L1_ROWS[c]):
            sel[:, (m % F + J_CHUNK * c + m // F) % F, SEL_L1 + c * COMMON_ROWS + m] = 1
    for m in range(COMMON_ROWS):
        sel[:, m % F, SEL_COMMON + m] = 1
    for m in range(F):
        sel[:, 2 * (m % L2_CHUNKS) + m // L2_CHUNKS, SEL_FIELDS + m] = 1
    return sel.reshape(FP, SEL_COLS)


def layer1_rows(w):
    w = w.reshape(F, F, H)
    a = np.zeros((L1_CHUNKS, J_CHUNK, F, H), w.dtype)
    b = np.zeros((L1_CHUNKS, J_CHUNK, F, H), w.dtype)
    for j in range(JS):
        for f in range(F):
            g = (f + j) % F
            a[j // J_CHUNK, j % J_CHUNK, f] = w[f, g]
            if 0 < j < F // 2:
                b[j // J_CHUNK, j % J_CHUNK, f] = w[g, f]
    return [np.ascontiguousarray(x.reshape(L1_CHUNKS, COMMON_ROWS, H).transpose(1, 0, 2)) for x in (a, b)]


def kernel(**inputs):
    import concourse.bacc as bacc
    from concourse.bass_utils import run_bass_kernel_spmd

    x = {k: np.asarray(v) for k, v in inputs.items()}
    w0a, w0b = layer1_rows(x["L0_rec_W0"])
    wt1 = x["W_top1"]
    group = np.arange(P)[:, None] % 8 == np.arange(8)[None, :]
    arrays = {
        "ids": x["ids"],
        "w0a": w0a,
        "w0b": w0b,
        "w1": x["L0_rec_W1"].reshape(L2_CHUNKS, P, H).transpose(1, 0, 2),
        "w2": x["L0_rec_W2"].reshape(L2_CHUNKS, P, H).transpose(1, 0, 2),
        "wt1a": wt1[H:3 * H],
        "wt1b": np.concatenate([wt1[0:H], wt1[3 * H:]]),
        "bt1": x["b_top1"].reshape(N1 // P, P).T,
        "wt2": x["W_top2"].reshape(N1 // P, P, N2).transpose(1, 0, 2),
        "bt2": x["b_top2"].reshape(N2 // P, P).T,
        "wt3": x["W_top3"].reshape(N2 // P, P).T,
        "dense_t": x["dense_ctx"].T,
        "sel": selectors(),
        "mask": group.astype(np.float32),
        "ident": np.eye(P, dtype=np.float32),
    }
    for f in range(F):
        arrays[f"tbl_{f}"] = x[f"tbl_{f}"]
    arrays = {k: np.ascontiguousarray(v) for k, v in arrays.items()}

    nc = bacc.Bacc("TRN2", target_bir_lowering=False, num_devices=1)
    ap = {k: nc.dram_tensor(f"in_{k}", v.shape, mybir.dt.from_np(v.dtype), kind="ExternalInput").ap()
          for k, v in arrays.items()}
    out = nc.dram_tensor("out_y", (B, 1), F32, kind="ExternalOutput").ap()
    build_tower(nc, ap["ids"], [ap[f"tbl_{f}"] for f in range(F)], ap["w0a"], ap["w0b"], ap["w1"],
                ap["w2"], ap["wt1a"], ap["wt1b"], ap["bt1"], ap["wt2"], ap["bt2"], ap["wt3"], ap["dense_t"],
                ap["sel"], ap["mask"], ap["ident"], out)
    got = run_bass_kernel_spmd(nc, [{f"in_{k}": v for k, v in arrays.items()}], core_ids=[0])
    return got.results[0]["out_y"]
```
